# Optimizing a Trainium2 kernel written in Bass

```python
import numpy as np
import jax
import jax.numpy as jnp

def _softmax(x, axis=-1):
    return jax.nn.softmax(x, axis=axis)

def _gelu(x):
    return jax.nn.gelu(x, approximate=True)

def _silu(x):
    return jax.nn.silu(x)

def _sigmoid(x):
    return jax.nn.sigmoid(x)

def _layernorm(x, axis=-1, eps=1e-05):
    m = jnp.mean(x, axis=axis, keepdims=True)
    v = jnp.var(x, axis=axis, keepdims=True)
    return (x - m) / jnp.sqrt(v + eps)

def _scatter_add(tgt, idx, src, axis=0):
    return tgt.at[idx].add(src)

def _segment_sum(src, seg, n):
    return jax.ops.segment_sum(src, seg, n)
kernel_name = 'mk_vit_tower_d1_tok_img256_r4_1b7fe9'

def setup_inputs(seed: int=0):
    np.random.seed(seed)
    _w = jnp.asarray

    def _rec_inputs():
        import jax
        import jax.numpy as jnp
        _rk = jax.random.key(seed)
        x = -7.10856e-05 + 0.999911 * jax.random.normal(jax.random.fold_in(_rk, 1), (16, 64, 128, 64), jnp.float32)
        return x
    x = _rec_inputs()

    def _L0_tok_setup():
        import jax, jax.numpy as jnp
        import numpy as np
        PATCH_LEN = 16
        STRIDE = 8
        PAD = 8
        key = jax.random.key(seed)
        k1, k2 = jax.random.split(key)
        x = jax.random.normal(k1, (32, 64, 128, 64), dtype=jnp.float32)
        in_feat = 64 * (PATCH_LEN // 2 + 1) * 2
        W = jax.random.normal(k2, (64, in_feat), dtype=jnp.float32) * 0.02
        return {'x': x, 'W': W}
    _L0_tok_all = _L0_tok_setup()
    _L0_tok_in = {k: v for k, v in _L0_tok_all.items() if k in ('W',)}
    del _L0_tok_all

    def _L0_attn_setup():
        import jax, jax.numpy as jnp
        import numpy as np
        D = 64
        L = 2
        B, S = (8, 1024)
        LR = 0.001
        WD = 0.01
        MAX_ALR = 0.1
        EPS = 1e-08

        def _lmm(Ws, bs, x):
            for i in range(L):
                x = x + jax.nn.silu(x @ Ws[i] + bs[i])
            return x

        def _reference_tuple_inner(x, Wk, Wq, Wv, Wlr, blr, Ws, bs):
            keys = x @ Wk
            queries = x @ Wq
            values = x @ Wv
            alr = (jax.nn.sigmoid(x @ Wlr + blr) * MAX_ALR).reshape(-1)

            def loss_fn(params):
                Ws_, bs_ = params
                preds = _lmm(Ws_, bs_, keys).reshape(-1, D)
                tgt = values.reshape(-1, D)
                per_tok = jnp.mean((preds - tgt) ** 2, axis=-1)
                return jnp.sum(per_tok * alr)
            gWs, gbs = jax.grad(loss_fn)((Ws, bs))

            def adamw_step(p, g):
                return p * (1.0 - LR * WD) - LR * g / (jnp.sqrt(g * g) + EPS)
            nWs = adamw_step(Ws, gWs)
            nbs = adamw_step(bs, gbs)
            retrieved = _lmm(nWs, nbs, queries)
            return (retrieved, -gWs, -gbs)
        key = jax.random.key(seed)
        ks = jax.random.split(key, 9)
        scale = 0.05
        return {'x': jax.random.normal(ks[0], (B, S, D), dtype=jnp.float32), 'Wk': jax.random.normal(ks[1], (D, D), dtype=jnp.float32) * scale, 'Wq': jax.random.normal(ks[2], (D, D), dtype=jnp.float32) * scale, 'Wv': jax.random.normal(ks[3], (D, D), dtype=jnp.float32) * scale, 'Wlr': jax.random.normal(ks[4], (D, 1), dtype=jnp.float32) * scale, 'blr': jnp.zeros((1,), dtype=jnp.float32), 'Ws': jax.random.normal(ks[5], (L, D, D), dtype=jnp.float32) * scale, 'bs': jnp.zeros((L, D), dtype=jnp.float32)}
    _L0_attn_all = _L0_attn_setup()
    _L0_attn_in = {k: v for k, v in _L0_attn_all.items() if k in ('Wk', 'Wq', 'Wv', 'Wlr', 'blr', 'Ws', 'bs')}
    del _L0_attn_all

    def _L0_ffn_setup():
        import jax, jax.numpy as jnp
        import numpy as np
        B, T, IN_DIM = (64, 64, 64)
        HID, OUT_DIM = (128, 64)
        N_LAYERS, N_EXPERTS, N_SHARED = (2, 16, 1)
        key = jax.random.key(seed)
        ks = jax.random.split(key, 10)
        s = 0.02
        x = jax.random.normal(ks[0], (B, T, IN_DIM), dtype=jnp.float32)
        route_id = jax.random.randint(ks[1], (B,), 0, N_EXPERTS)
        Wi = jax.random.normal(ks[2], (HID, IN_DIM), dtype=jnp.float32) * s
        bi = jnp.zeros((HID,), dtype=jnp.float32)
        Wr = jax.random.normal(ks[3], (N_LAYERS, N_EXPERTS, HID, HID), dtype=jnp.float32) * s
        br = jax.random.normal(ks[4], (N_LAYERS, N_EXPERTS, HID), dtype=jnp.float32) * s
        Ws = jax.random.normal(ks[5], (N_LAYERS, N_SHARED, HID, HID), dtype=jnp.float32) * s
        bs = jax.random.normal(ks[6], (N_LAYERS, N_SHARED, HID), dtype=jnp.float32) * s
        Wo = jax.random.normal(ks[7], (OUT_DIM, HID), dtype=jnp.float32) * s
        bo = jnp.zeros((OUT_DIM,), dtype=jnp.float32)
        return {'x': x, 'route_id': route_id, 'Wi': Wi, 'bi': bi, 'Wr': Wr, 'br': br, 'Ws': Ws, 'bs': bs, 'Wo': Wo, 'bo': bo}
    _L0_ffn_all = _L0_ffn_setup()
    _L0_ffn_in = {k: v for k, v in _L0_ffn_all.items() if k in ('route_id', 'Wi', 'bi', 'Wr', 'br', 'Ws', 'bs', 'Wo', 'bo')}
    del _L0_ffn_all
    return {'x': x, 'L0_tok_W': _L0_tok_in['W'], 'L0_attn_Wk': _L0_attn_in['Wk'], 'L0_attn_Wq': _L0_attn_in['Wq'], 'L0_attn_Wv': _L0_attn_in['Wv'], 'L0_attn_Wlr': _L0_attn_in['Wlr'], 'L0_attn_blr': _L0_attn_in['blr'], 'L0_attn_Ws': _L0_attn_in['Ws'], 'L0_attn_bs': _L0_attn_in['bs'], 'L0_ffn_route_id': _L0_ffn_in['route_id'], 'L0_ffn_Wi': _L0_ffn_in['Wi'], 'L0_ffn_bi': _L0_ffn_in['bi'], 'L0_ffn_Wr': _L0_ffn_in['Wr'], 'L0_ffn_br': _L0_ffn_in['br'], 'L0_ffn_Ws': _L0_ffn_in['Ws'], 'L0_ffn_bs': _L0_ffn_in['bs'], 'L0_ffn_Wo': _L0_ffn_in['Wo'], 'L0_ffn_bo': _L0_ffn_in['bo']}

def reference(x, L0_tok_W, L0_attn_Wk, L0_attn_Wq, L0_attn_Wv, L0_attn_Wlr, L0_attn_blr, L0_attn_Ws, L0_attn_bs, L0_ffn_route_id, L0_ffn_Wi, L0_ffn_bi, L0_ffn_Wr, L0_ffn_br, L0_ffn_Ws, L0_ffn_bs, L0_ffn_Wo, L0_ffn_bo):
    import jax
    import jax.numpy as jnp

    def _L0_tok_ref(x, W):
        import jax, jax.numpy as jnp
        import numpy as np
        PATCH_LEN = 16
        STRIDE = 8
        PAD = 8
        B, C, T, V = x.shape
        xp = jnp.pad(x, ((0, 0), (0, 0), (0, PAD), (0, 0)), mode='edge')
        Tp = T + PAD
        N = (Tp - PATCH_LEN) // STRIDE + 1
        idx = jnp.arange(N)[:, None] * STRIDE + jnp.arange(PATCH_LEN)[None, :]
        patches = xp[:, :, idx, :]
        patches = jnp.transpose(patches, (0, 4, 2, 3, 1))
        xf = jnp.fft.rfft(patches, axis=-2, norm='ortho')
        F = xf.shape[-2]
        x_real = xf.real.reshape(B, V, N, F * C)
        x_imag = xf.imag.reshape(B, V, N, F * C)
        x_emb = jnp.concatenate([x_real, x_imag], axis=-1)
        x_emb = x_emb @ W.T
        return x_emb.reshape(B, V * N, -1)

    def _L0_attn_ref(x, Wk, Wq, Wv, Wlr, blr, Ws, bs):
        import jax, jax.numpy as jnp
        import numpy as np
        D = 64
        L = 2
        B, S = (8, 1024)
        LR = 0.001
        WD = 0.01
        MAX_ALR = 0.1
        EPS = 1e-08

        def _lmm(Ws, bs, x):
            for i in range(L):
                x = x + jax.nn.silu(x @ Ws[i] + bs[i])
            return x

        def _reference_tuple_inner(x, Wk, Wq, Wv, Wlr, blr, Ws, bs):
            keys = x @ Wk
            queries = x @ Wq
            values = x @ Wv
            alr = (jax.nn.sigmoid(x @ Wlr + blr) * MAX_ALR).reshape(-1)

            def loss_fn(params):
                Ws_, bs_ = params
                preds = _lmm(Ws_, bs_, keys).reshape(-1, D)
                tgt = values.reshape(-1, D)
                per_tok = jnp.mean((preds - tgt) ** 2, axis=-1)
                return jnp.sum(per_tok * alr)
            gWs, gbs = jax.grad(loss_fn)((Ws, bs))

            def adamw_step(p, g):
                return p * (1.0 - LR * WD) - LR * g / (jnp.sqrt(g * g) + EPS)
            nWs = adamw_step(Ws, gWs)
            nbs = adamw_step(bs, gbs)
            retrieved = _lmm(nWs, nbs, queries)
            return (retrieved, -gWs, -gbs)
        return _reference_tuple_inner(x, Wk, Wq, Wv, Wlr, blr, Ws, bs)[0]

    def _L0_ffn_ref(x, route_id, Wi, bi, Wr, br, Ws, bs, Wo, bo):
        import jax, jax.numpy as jnp
        import numpy as np
        B, T, IN_DIM = (64, 64, 64)
        HID, OUT_DIM = (128, 64)
        N_LAYERS, N_EXPERTS, N_SHARED = (2, 16, 1)
        flat = x.reshape(-1, x.shape[-1])
        n_tok = flat.shape[0]
        route = jnp.repeat(route_id, n_tok // route_id.shape[0])
        h = jax.nn.relu(flat @ Wi.T + bi)
        n_layers, n_experts = (Wr.shape[0], Wr.shape[1])
        for l in range(n_layers):
            shared = (jnp.einsum('nd,shd->snh', h, Ws[l]) + bs[l][:, None, :]).mean(axis=0)
            routed = jnp.zeros_like(h)
            for e in range(n_experts):
                ye = h @ Wr[l, e].T + br[l, e]
                routed = routed + jnp.where((route == e)[:, None], ye, 0.0)
            h = jax.nn.relu(shared + routed + h)
        out = h @ Wo.T + bo
        return out.reshape(*x.shape[:-1], out.shape[-1])
    h = _L0_tok_ref(x, L0_tok_W)
    h = h + _L0_attn_ref(_layernorm(h, axis=-1), L0_attn_Wk, L0_attn_Wq, L0_attn_Wv, L0_attn_Wlr, L0_attn_blr, L0_attn_Ws, L0_attn_bs)
    h = h + _L0_ffn_ref(_layernorm(h, axis=-1), L0_ffn_route_id, L0_ffn_Wi, L0_ffn_bi, L0_ffn_Wr, L0_ffn_br, L0_ffn_Ws, L0_ffn_bs, L0_ffn_Wo, L0_ffn_bo)
    return h

_drawn_inputs = setup_inputs


def setup_inputs(seed=0):
    import zlib

    import numpy as np

    out = dict(_drawn_inputs(seed))
    spreads = {'L0_attn_bs': (0.0, 0.1), 'L0_ffn_bi': (0.0, 0.312), 'L0_ffn_bo': (0.0, 0.1)}
    factors = {'L0_attn_Wk': 8.0,
     'L0_attn_Wv': 8.0,
     'L0_attn_Wlr': 8.0,
     'L0_ffn_Wr': 4.165,
     'L0_ffn_br': 7.428,
     'L0_ffn_Ws': 4.192,
     'L0_ffn_bs': 6.85}
    for name, (base, spread) in spreads.items():
        noise = np.random.default_rng([zlib.crc32(name.encode()), seed]).standard_normal(out[name].shape)
        drawn = base * np.exp(spread * noise) if base else spread * noise
        out[name] = jnp.asarray(drawn.astype(out[name].dtype))
    for name, factor in factors.items():
        out[name] = (out[name] * factor).astype(out[name].dtype)
    return out
```

```python
from contextlib import ExitStack

import numpy as np

import concourse.bass as bass
from concourse import mybir

F32 = mybir.dt.float32
I32 = mybir.dt.int32
ALU = mybir.AluOpType
ACT = mybir.ActivationFunctionType

B, C, T, V = 16, 64, 128, 64
D = 64
PATCH, STRIDE = 16, 8
NP = T // STRIDE
NJ = NP // 2
COLS = NJ * V
TILES = COLS // 128
HALF = STRIDE // 2
HID, EXPERTS, LAYERS = 128, 16, 2
GROUPS = 4
GV = V // GROUPS
GC = NP * GV
XW = 2 * D + 1
WE = HID + 1
LR, WD, MAX_ALR, ADAM_EPS, LN_EPS = 1e-3, 0.01, 0.1, 1e-8, 1e-5

PACK = [
    ("wk_bd", 128), ("wv_bd", 128), ("wq_bd", 128), ("w1_bd", 128), ("w1t_bd", 128),
    ("wkt_dd", 128), ("wqt_dd", 128), ("grad0", 128), ("grad1", 128),
    ("w0_dd", 64), ("w1_dd", 64), ("b0_dd", 1), ("b1_dd", 1),
    ("wlr", 2), ("blr", 1), ("wit_dd", 128), ("bi", 1),
    ("ws0", WE), ("ws1", WE), ("wot", 64), ("bo", 64),
    ("ident", 128), ("center", 128), ("mean", 128), ("spread0", 128), ("spread1", 128),
]
AT = {}
_at = 0
for _name, _w in PACK:
    AT[_name] = (_at, _at + _w)
    _at += _w
PACKED = _at

EVEN = [(0, f) for f in range(0, 9, 2)] + [(1, f) for f in range(2, 8, 2)]
ODD = [(0, f) for f in range(1, 9, 2)] + [(1, f) for f in range(1, 9, 2)]
ROUNDS = len(EVEN)


def dft(part, f, k):
    a = 2 * np.pi * f * k / PATCH
    return (np.cos(a) if part == 0 else -np.sin(a)) / np.sqrt(PATCH)


def fold_table():
    t = np.zeros((128, ROUNDS, 2, HALF + 1))
    for n in range(ROUNDS):
        for parity, (part, f) in enumerate((EVEN[n], ODD[n])):
            for h in range(2):
                for k in range(HALF):
                    t[64 * h:64 * h + 64, n, parity, k] = dft(part, f, HALF * h + k)
            tail = sum(dft(part, f, k) for k in range(STRIDE, PATCH))
            t[:, n, parity, HALF] = 0.0 if abs(tail) < 1e-9 else tail
    return t.astype(np.float32)


FRONT = 4


def steps(eng, lag, unroll, step, front=FRONT):
    for i in range(front):
        step(i, i % unroll)
    with eng.Fori(0, (B - front) // unroll) as n:
        for k in range(unroll):
            step(n * unroll + front + k, (front + k) % unroll)
    for i in range(B, B + lag):
        step(i, i % unroll)


def real(c, n=B):
    return not isinstance(c, int) or 0 <= c < n


def since(c, first):
    return not isinstance(c, int) or c >= first


def tower(nc, x, tokw, fold, pack, experts, route, out):
    ctx = ExitStack()
    with ctx:
        def sb(name, shape, dt=F32):
            return ctx.enter_context(nc.sbuf_tensor(name, shape, dt))

        def sem(name):
            return ctx.enter_context(nc.semaphore(name))

        hT = sb("hT", [128, B * COLS])
        xT = sb("xT", [128, B * COLS])
        rows = sb("rows", [128, B * TILES * 2 * XW])
        W = sb("W", [128, PACKED])
        w = {n: W[:, a:b] for n, (a, b) in AT.items()}
        tokw_sb = xT[:, B * COLS - 18 * D:].rearrange("p (f o) -> p f o", o=D)
        fold_sb = sb("fold_sb", [128, ROUNDS, 2, HALF + 1])
        patch_w = sb("patch_w", [128, HALF, 3, D])
        patch_end = sb("patch_end", [128, 2 * D])
        z_w = sb("z_w", [128, 2, 128])
        d_w = sb("d_w", [128, 128])
        r_w = sb("r_w", [128, 2, 128])
        n1_bd = sb("n1_bd", [128, 128])
        wi_p = sb("wi_p", [128, 2, 128])
        logit = sb("logit", [128, B * TILES * 2])
        alr = sb("alr", [128, B * TILES * 2, 1])
        half_b = sb("half_b", [128, 3])
        eps = sb("eps", [128, 1])
        grad_s = sb("grad_s", [128, XW])
        gradt_s = sb("gradt_s", [128, 128])
        adam = sb("adam", [128, 3, 130])
        params = sb("params", [128, 130])
        route_sb = sb("route_sb", [1, B * GROUPS], I32)
        route_f = sb("route_f", [1, 4, B * GROUPS])
        route_ix = sb("route_ix", [1, B * GROUPS], I32)

        arena = sb("arena", [128, 13 * 1024])
        at = [0]

        def scratch(*shape):
            n = int(np.prod(shape))
            a = arena[:, at[0]:at[0] + n]
            at[0] += n
            if len(shape) == 2:
                return a.rearrange("p (a b) -> p a b", b=shape[1])
            if len(shape) == 3:
                return a.rearrange("p (a b c) -> p a b c", b=shape[1], c=shape[2])
            return a

        xb = scratch(2, 2 * NJ, HALF * V)
        odd_s = scratch(2, COLS)
        sq = scratch(2, COLS)
        std = scratch(2, COLS)
        rstd = scratch(2, COLS)
        xh = scratch(2, COLS)
        at[0] = 0
        s0, c0, s1, c1, dd, dz0 = (scratch(2, COLS) for _ in range(6))
        dzt = scratch(2, 2 * TILES, 2 * D)
        at[0] = 0
        p0, p1, hs = (scratch(2, COLS) for _ in range(3))
        h2 = scratch(2, NJ, 2 * V)
        at[0] = 0
        sq2, std2, rstd2, x2 = (scratch(2, COLS) for _ in range(4))
        hid0, hid1 = (scratch(NP * V) for _ in range(2))
        hidF = scratch(2, NP, 2 * V)
        outs = scratch(2, NP * D)
        resid = rows[:, 0:B // 2 * NP * D]
        e0 = B // 2 * NP * D
        e1 = e0 + LAYERS * (EXPERTS + 1) * WE
        wr = rows[:, e0:e1].rearrange("p (l e n) -> p l e n", l=LAYERS, n=WE)
        e2 = e1 + LAYERS * 2 * GROUPS * WE
        assert e2 <= B * TILES * 2 * XW
        wuse = rows[:, e1:e2].rearrange("p (l s n) -> p l s n", l=LAYERS, n=WE)
        rows3 = rows[:, :].rearrange("p (t n) -> p t n", n=XW)

        bank = [ctx.enter_context(nc.psum_tensor(f"bank{n}", [128, COLS], F32)) for n in range(8)]

        def by(ap, n):
            return ap.rearrange("p (a n) -> p a n", n=n)

        x_in = [sem("x_in0"), sem("x_in1")]
        w_in, tokw_in, wr_in, route_in = sem("w_in"), sem("tokw_in"), sem("wr_in"), sem("route_in")
        zeroed, folded, setup_pe, setup_act, setup_pool = (
            sem(n) for n in ("zeroed", "folded", "setup_pe", "setup_act", "setup_pool"))
        odd_done, even_done, odd_out, added, centred, squared, var_done, rooted, rstd_done = (
            sem(n) for n in ("odd_done", "even_done", "odd_out", "added", "centred", "squared",
                             "var_done", "rooted", "rstd_done"))
        normed, stored, turned, turned_out = (sem(n) for n in ("normed", "stored", "turned", "turned_out"))
        alr_t, alr_done = sem("alr_t"), sem("alr_done")
        z0_done, d_done, z1_done, s0_done, t0_done, s1_done, t1_done = (
            sem(n) for n in ("z0_done", "d_done", "z1_done", "s0_done", "t0_done", "s1_done", "t1_done"))
        m0_done, c0_done, m1_done, c1_done, ss_done, dd_done, dz1_done = (
            sem(n) for n in ("m0_done", "c0_done", "m1_done", "c1_done", "ss_done", "dd_done", "dz1_done"))
        back_done, dy_done, dz0_done, s0t_done, s0t_out, dz1t_done, dz1t_out, dz0t_done, dz0t_out = (
            sem(n) for n in ("back_done", "dy_done", "dz0_done", "s0t_done", "s0t_out", "dz1t_done",
                             "dz1t_out", "dz0t_done", "dz0t_out"))
        gw_done, learn_pe, learn_dve = sem("gw_done"), sem("learn_pe"), sem("learn_dve")
        rz0_done, rq_done, rz1_done, p0_done, p1_done, hs_done, hq_done, h2_done, h2_stored = (
            sem(n) for n in ("rz0_done", "rq_done", "rz1_done", "p0_done", "p1_done", "hs_done",
                             "hq_done", "h2_done", "h2_stored"))
        h2t_done, h2t_out = sem("h2t_done"), sem("h2t_out")
        c2_done, sq2_done, v2_done, std2_done, rstd2_done, x2_done = (
            sem(n) for n in ("c2_done", "sq2_done", "v2_done", "std2_done", "rstd2_done", "x2_done"))
        in_done, l1_done, l2_done, h0_ready, h1_ready, hF_ready = (
            sem(n) for n in ("in_done", "l1_done", "l2_done", "h0_ready", "h1_ready", "hF_ready"))
        wo_done, out_added, wuse_ready, route_step = (
            sem(n) for n in ("wo_done", "out_added", "wuse_ready", "route_step"))
        out_dma = [sem("out_dma0"), sem("out_dma1")]

        P_ODD, P_EVEN, P_C, P_V, P_T, P_L = bank[0:2], bank[2], bank[3:5], bank[5], bank[6], bank[7]
        A_Z0, A_Z1, A_D, A_BACK, A_S0T, A_DZ1T, A_DZ0T, A_G = bank
        R_Z0, R_Z1, R_Q, R_T = bank[0], bank[1], bank[2], bank[4:6]
        E_H, E_C, E_V, E_O = bank[0:4], bank[4], bank[5], bank[6:8]

        xs = x.rearrange("b c (m h t) v -> b h c m (t v)", h=2, t=HALF)
        out_rows = out.rearrange("b (v n) d -> (b v) (n d)", n=NP)

        def cols(tensor, c, n=COLS):
            return tensor[:, bass.ds(c * n, n)]

        def h2_of(k):
            return h2[:, k // 2].rearrange("p j (b v) -> p b j v", b=2)[:, k % 2]

        block = ctx.enter_context(nc.Block())

        @block.sync
        def _(sp):
            def load_x(i, k):
                if since(i, 2):
                    sp.wait_ge(even_done, i - 1)
                for h in range(2):
                    sp.dma_start(xb[64 * h:64 * h + 64, k], xs[bass.ds(i, 1), h].rearrange("o c m n -> c (o m) n")
                                 ).then_inc(x_in[k], 16)

            sp.dma_start(tokw_sb[0:64], tokw).then_inc(tokw_in, 16)
            sp.dma_start(tokw_sb[64:128], tokw).then_inc(tokw_in, 16)
            sp.dma_start(fold_sb[:], fold).then_inc(tokw_in, 16)
            load_x(0, 0)
            sp.dma_start(W[:, :], pack).then_inc(w_in, 16)
            load_x(1, 1)
            sp.dma_start(route_sb[:], route).then_inc(route_in, 16)
            with sp.Fori(1, B // 2) as n:
                for k in range(2):
                    load_x(2 * n + k, k)
            sp.wait_ge(gw_done, B)
            sp.dma_start(rows[:, e0:e1], experts).then_inc(wr_in, 16)

            def store(p, s, row):
                sp.wait_ge(out_added, 2 * p + 2)
                sp.dma_start(out_rows[bass.ds(row, 128), :], outs[:, s]).then_inc(out_dma[s], 16)

            with sp.Fori(0, B // 4) as n:
                for s in range(2):
                    store(2 * n + s, s, n * 256 + s * 128)
            for s in range(2):
                sp.wait_ge(out_dma[s], 16 * (B // 4))

        @block.tensor
        def _(pe):
            mm, tr = nc.tensor.matmul, nc.tensor.transpose

            pe.wait_ge(w_in, 16)
            mm(P_L[:, 0:64], w["wkt_dd"][0:64], w["w0_dd"][0:64], start=True, stop=True)
            mm(P_L[:, 64:128], w["wkt_dd"][0:64], w["w1_dd"][0:64], start=True, stop=True)
            mm(P_L[:, 128:256], w["center"], w["wit_dd"], start=True, stop=True).then_inc(setup_pe, 1)

            pe.wait_ge(folded, ROUNDS + 3)
            pe.wait_ge(setup_act, 1)

            def tokenize(i, k):
                k = k % 2
                if real(i):
                    pe.wait_ge(x_in[k], 16 * (i - k) + 32)
                    if since(i, 2):
                        pe.wait_ge(added, i - 1)
                    xm = xb[:, k].rearrange("p (j o) (t v) -> p j o t v", o=2, t=HALF)
                    for t in (0, HALF - 1, *range(1, HALF - 1)):
                        lhs = patch_w[:, t, 0:2].rearrange("p a b -> p (a b)")
                        if t < HALF - 1:
                            last = mm(P_ODD[k][:, :], lhs, xm[:, :, 1, t], start=(t == 0), stop=(t == HALF - 2))
                        else:
                            mm(P_ODD[k][:, 0:COLS - V], lhs, xm[:, 0:NJ - 1, 1, t], start=False, stop=False,
                               skip_group_check=True)
                            mm(P_ODD[k][:, COLS - V:], patch_end[:, :], xm[:, NJ - 1, 1, t], start=False,
                               stop=False, skip_group_check=True)
                    last.then_inc(odd_done, 1)
                if real(i - 1):
                    pe.wait_ge(added, i)
                    if since(i, 3):
                        pe.wait_ge(normed, i - 2)
                    mm(P_C[1 - k][:, :], w["center"], cols(hT, i - 1), start=True, stop=True).then_inc(centred, 1)
                if real(i):
                    if since(i, 1):
                        pe.wait_ge(odd_out, i)
                    for t in range(HALF):
                        last = mm(P_EVEN[:, :], patch_w[:, t, 1:3].rearrange("p a b -> p (a b)"),
                                  xm[:, :, 0, t], start=(t == 0), stop=(t == HALF - 1))
                    last.then_inc(even_done, 1)
                if real(i - 1):
                    pe.wait_ge(squared, i)
                    if since(i, 2):
                        pe.wait_ge(rooted, i - 1)
                    mm(P_V[:, :], w["mean"], sq[:, 1 - k], start=True, stop=True).then_inc(var_done, 1)
                if real(i - 2):
                    pe.wait_ge(normed, i - 1)
                    if since(i, 3):
                        pe.wait_ge(turned_out, i - 2)
                    for t in range(TILES):
                        tile = xh[:, k, 128 * t:128 * t + 128]
                        tr(P_T[:, 128 * t:128 * t + 128], tile, w["ident"])
                        last = mm(P_L[:, 2 * t:2 * t + 2], tile, w["wlr"], start=True, stop=True)
                    last.then_inc(turned, 1)

            steps(pe, 2, 2, tokenize)

            pe.wait_ge(stored, B)
            pe.wait_ge(turned_out, B)
            pe.wait_ge(normed, B)
            pe.wait_ge(setup_pool, 1)

            def learn(i, k):
                other = 1 - k
                if real(i):
                    if since(i, 1):
                        pe.wait_ge(t0_done, i)
                    mm(A_Z0[:, :], z_w[:, 0], cols(xT, i), start=True, stop=True).then_inc(z0_done, 1)
                    if since(i, 1):
                        pe.wait_ge(dd_done, i)
                    mm(A_D[:, :], d_w[:, :], cols(xT, i), start=True, stop=True).then_inc(d_done, 1)
                    if since(i, 1):
                        pe.wait_ge(t1_done, i)
                    mm(A_Z1[:, :], z_w[:, 1], cols(xT, i), start=True, stop=False)
                if real(i - 3):
                    pe.wait_ge(s0t_out, i - 2)
                    pe.wait_ge(dz0t_out, i - 2)
                    pe.wait_ge(dz1t_out, i - 2)
                    for t in range(2 * TILES):
                        first = isinstance(i, int) and i == 3 and t == 0
                        final = isinstance(i, int) and i == B + 2 and t == 2 * TILES - 1
                        last = mm(A_G[:, 0:XW], dzt[:, other, t], cols(rows, (i - 3) * 2 * TILES + t, XW),
                                  start=first, stop=final, skip_group_check=True)
                    last.then_inc(gw_done, 1)
                if real(i - 1):
                    if since(i, 2):
                        pe.wait_ge(s0t_out, i - 1)
                    for t in range(TILES):
                        tile = slice(128 * t, 128 * t + 128)
                        last = tr(A_S0T[:, tile], s0[:, other, tile], w["ident"])
                    last.then_inc(s0t_done, 1)
                if real(i):
                    pe.wait_ge(s0_done, i + 1)
                    mm(A_Z1[:, :], w["w1_bd"], s0[:, k], start=False, stop=True).then_inc(z1_done, 1)
                if real(i - 1):
                    pe.wait_ge(dz1_done, i)
                    if since(i, 2):
                        pe.wait_ge(dy_done, i - 1)
                    mm(A_BACK[:, :], w["w1t_bd"], c1[:, other], start=True, stop=True).then_inc(back_done, 1)
                    if since(i, 2):
                        pe.wait_ge(dz1t_out, i - 1)
                    for t in range(TILES):
                        tile = slice(128 * t, 128 * t + 128)
                        last = tr(A_DZ1T[:, tile], c1[:, other, tile], w["ident"])
                    last.then_inc(dz1t_done, 1)
                if real(i - 2):
                    pe.wait_ge(dz0_done, i - 1)
                    if since(i, 3):
                        pe.wait_ge(dz0t_out, i - 2)
                    for t in range(TILES):
                        tile = slice(128 * t, 128 * t + 128)
                        last = tr(A_DZ0T[:, tile], dz0[:, k, tile], w["ident"])
                    last.then_inc(dz0t_done, 1)

            steps(pe, 3, 2, learn)

            pe.wait_ge(learn_dve, 1)
            tr(A_Z0[:, 0:128], grad_s[:, 0:128], w["ident"]).then_inc(learn_pe, 1)
            mm(A_Z1[:, 128:129], w["spread0"], grad_s[:, 128:129], start=True, stop=True)
            mm(A_Z1[:, 129:130], w["spread1"], grad_s[:, 128:129], start=True, stop=True)
            pe.wait_ge(learn_dve, 2)
            mm(A_Z1[:, 0:64], w["grad0"], gradt_s[:, 0:64], start=True, stop=True)
            mm(A_Z1[:, 64:128], w["grad1"], gradt_s[:, 64:128], start=True, stop=True).then_inc(learn_pe, 1)
            pe.wait_ge(learn_dve, 8)
            mm(A_D[:, 0:128], w["wqt_dd"][0:64], params[0:64, 0:128], start=True, stop=True).then_inc(learn_pe, 1)
            pe.wait_ge(learn_dve, 12)

            def retrieve(i, k):
                if real(i):
                    if since(i, 1):
                        pe.wait_ge(p0_done, i)
                    mm(R_Z0[:, :], r_w[:, 0], cols(xT, i), start=True, stop=True).then_inc(rz0_done, 1)
                    if since(i, 1):
                        pe.wait_ge(hq_done, i)
                    mm(R_Q[:, :], w["wq_bd"], cols(xT, i), start=True, stop=True).then_inc(rq_done, 1)
                    if since(i, 1):
                        pe.wait_ge(p1_done, i)
                    mm(R_Z1[:, :], r_w[:, 1], cols(xT, i), start=True, stop=False)
                    pe.wait_ge(p0_done, i + 1)
                    mm(R_Z1[:, :], n1_bd[:, :], p0[:, k % 2], start=False, stop=True).then_inc(rz1_done, 1)
                if k % 2 == 0 and since(i, 2):
                    pe.wait_ge(h2_done, i)
                    if since(i, 4):
                        pe.wait_ge(h2t_out, i - 2)
                    pair = ((k - 2) % 4) // 2
                    for q in range(2):
                        for j in range(NJ // 2):
                            last = tr(R_T[q][:, 128 * j:128 * j + 128], h2[:, pair, q * NJ // 2 + j], w["ident"])
                        last.then_inc(h2t_done, 1)

            steps(pe, 1, 4, retrieve)

            pe.wait_ge(h2_stored, B)
            pe.wait_ge(h2t_out, B)

            def route_experts(i, k):
                par = k % 2
                first, second = 2 * par, 2 * (1 - par)
                if real(i - 2):
                    pe.wait_ge(x2_done, i - 1)
                    if since(i, 3):
                        pe.wait_ge(h1_ready, 2 * i - 4)
                    xv = x2[:, par].rearrange("p (j g v) -> p g j v", g=GROUPS, v=GV)
                    for b in range(2):
                        hv = E_H[first + b][:, :].rearrange("p (g r j v) -> p r g j v", g=2, r=2, v=GV)
                        for r in range(2):
                            last = mm(hv[:, r], wi_p[:, r], xv[:, 2 * b:2 * b + 2], start=True, stop=True)
                        last.then_inc(in_done, 1)
                if real(i):
                    if since(i, 1):
                        pe.wait_ge(sq2_done, i)
                    mm(E_C[:, :], w["center"], cols(hT, i), start=True, stop=True).then_inc(c2_done, 1)
                if par == 0 and since(i, 4):
                    pe.wait_ge(hF_ready, 2 * i - 4)
                    if since(i, 6):
                        pe.wait_ge(out_added, i - 4)
                    for n in range(NP):
                        last = mm(E_O[n // NJ][:, n % NJ * D:(n % NJ + 1) * D], hidF[:, k // 2, n], w["wot"],
                                  start=True, stop=True)
                        if n % NJ == NJ - 1:
                            last.then_inc(wo_done, 1)
                if real(i - 2):
                    pe.wait_ge(wuse_ready, i - 1)
                    if since(i, 3):
                        pe.wait_ge(hF_ready, 2 * i - 4)
                    for b in range(2):
                        pe.wait_ge(h0_ready, 2 * i - 3 + b)
                        for g in range(2 * b, 2 * b + 2):
                            last = mm(E_H[second + b][:, (g % 2) * GC:(g % 2 + 1) * GC], wuse[:, 0, par * GROUPS + g, 0:HID],
                                      hid0[:, g * GC:(g + 1) * GC], start=True, stop=True)
                        last.then_inc(l1_done, 1)
                if real(i):
                    pe.wait_ge(sq2_done, i + 1)
                    if since(i, 1):
                        pe.wait_ge(std2_done, i)
                    mm(E_V[:, :], w["mean"], sq2[:, par], start=True, stop=True).then_inc(v2_done, 1)
                if real(i - 2):
                    for b in range(2):
                        pe.wait_ge(h1_ready, 2 * i - 3 + b)
                        for g in range(2 * b, 2 * b + 2):
                            last = mm(E_H[first + b][:, (g % 2) * GC:(g % 2 + 1) * GC], wuse[:, 1, par * GROUPS + g, 0:HID],
                                      hid1[:, g * GC:(g + 1) * GC], start=True, stop=True)
                        last.then_inc(l2_done, 1)

            steps(pe, 3, 4, route_experts, 2 * FRONT)

        @block.scalar
        def _(act):
            f = nc.scalar.activation

            act.wait_ge(setup_pe, 1)
            act.wait_ge(zeroed, 1)
            for h in range(2):
                part = slice(64 * h, 64 * h + 64)
                f(z_w[part, :, 64 * h:64 * h + 64], by(P_L[part, 0:128], 64), ACT.Copy)
                last = f(wi_p[part, h], P_L[part, 128:256], ACT.Copy)
            last.then_inc(setup_act, 1)

            def tokenize(i, k):
                other = 1 - k
                if real(i - 1):
                    act.wait_ge(centred, i)
                    if since(i, 3):
                        act.wait_ge(var_done, i - 2)
                    f(sq[:, other], P_C[other][:, :], ACT.Square).then_inc(squared, 1)
                if real(i):
                    act.wait_ge(even_done, i + 1)
                    if since(i, 2):
                        act.wait_ge(added, i - 1)
                    f(odd_s[0:64, k], P_EVEN[0:64, :], ACT.Copy)
                    f(odd_s[64:128, k, 0:COLS - V], P_EVEN[64:128, V:], ACT.Copy).then_inc(odd_out, 1)
                if real(i - 1):
                    act.wait_ge(var_done, i)
                    if since(i, 3):
                        act.wait_ge(rstd_done, i - 2)
                    f(std[:, other], P_V[:, :], ACT.Sqrt, bias=eps[:, 0:1]).then_inc(rooted, 1)
                if real(i - 2):
                    act.wait_ge(turned, i - 1)
                    f(rows3[:, bass.ds((i - 2) * 2 * TILES, 2 * TILES), 0:D], by(P_T[:, :], D), ACT.Copy)
                    f(cols(logit, i - 2, 2 * TILES), P_L[:, 0:2 * TILES], ACT.Copy).then_inc(turned_out, 1)

            act.wait_ge(setup_pool, 1)
            steps(act, 2, 2, tokenize)

            act.wait_ge(turned_out, B)
            f(alr[:, :, 0], logit[:, :], ACT.Tanh, bias=half_b[:, 2:3], scale=0.5).then_inc(alr_t, 1)

            def learn(i, k):
                other = 1 - k
                if real(i):
                    act.wait_ge(z0_done, i + 1)
                    if since(i, 2):
                        act.wait_ge(s0t_done, i - 1)
                        act.wait_ge(z1_done, i - 1)
                        act.wait_ge(c0_done, i - 1)
                        act.wait_ge(dz0_done, i - 1)
                        act.wait_ge(ss_done, i - 1)
                    f(s0[:, k], A_Z0[:, :], ACT.Silu, bias=w["b0_dd"]).then_inc(s0_done, 1)
                    f(c0[:, k], A_Z0[:, :], ACT.Tanh, bias=half_b[:, 0:1], scale=0.5).then_inc(t0_done, 1)
                if real(i - 1):
                    act.wait_ge(s0t_done, i)
                    f(rows3[:, bass.ds((i - 1) * 2 * TILES, 2 * TILES), D:2 * D], by(A_S0T[:, :], D), ACT.Copy
                      ).then_inc(s0t_out, 1)
                if real(i):
                    act.wait_ge(z1_done, i + 1)
                    if since(i, 2):
                        act.wait_ge(c1_done, i - 1)
                        act.wait_ge(dz1t_done, i - 1)
                    f(s1[:, k], A_Z1[:, :], ACT.Silu, bias=w["b1_dd"]).then_inc(s1_done, 1)
                    f(c1[:, k], A_Z1[:, :], ACT.Tanh, bias=half_b[:, 1:2], scale=0.5).then_inc(t1_done, 1)

            steps(act, 1, 2, learn)

            def retrieve(i, k):
                k = k % 2
                if real(i):
                    act.wait_ge(rz0_done, i + 1)
                    if since(i, 2):
                        act.wait_ge(hs_done, i - 1)
                        act.wait_ge(rz1_done, i - 1)
                    f(p0[:, k], R_Z0[:, :], ACT.Silu, bias=params[:, 128:129]).then_inc(p0_done, 1)
                    act.wait_ge(rz1_done, i + 1)
                    if since(i, 2):
                        act.wait_ge(h2_done, i - 1)
                    f(p1[:, k], R_Z1[:, :], ACT.Silu, bias=params[:, 129:130]).then_inc(p1_done, 1)

            steps(act, 0, 2, retrieve)

            act.wait_ge(h2_stored, B)
            act.wait_ge(h2t_done, B)

            def route_experts(i, k):
                par = k % 2
                first, second = 2 * par, 2 * (1 - par)
                if real(i - 2):
                    if since(i, 3):
                        act.wait_ge(l1_done, 2 * i - 4)
                    for b in range(2):
                        act.wait_ge(in_done, 2 * i - 3 + b)
                        f(hid0[:, b * COLS:(b + 1) * COLS], E_H[first + b][:, :], ACT.Relu, bias=w["bi"]
                          ).then_inc(h0_ready, 1)
                if real(i):
                    act.wait_ge(c2_done, i + 1)
                    if since(i, 2):
                        act.wait_ge(v2_done, i - 1)
                    f(sq2[:, par], E_C[:, :], ACT.Square).then_inc(sq2_done, 1)
                if real(i - 2):
                    if since(i, 3):
                        act.wait_ge(l2_done, 2 * i - 4)
                    for b in range(2):
                        act.wait_ge(l1_done, 2 * i - 3 + b)
                        for g in range(2 * b, 2 * b + 2):
                            last = f(hid1[:, g * GC:(g + 1) * GC], E_H[second + b][:, (g % 2) * GC:(g % 2 + 1) * GC],
                                     ACT.Relu, bias=wuse[:, 0, par * GROUPS + g, HID:WE])
                        last.then_inc(h1_ready, 1)
                if real(i):
                    act.wait_ge(v2_done, i + 1)
                    if since(i, 2):
                        act.wait_ge(rstd2_done, i - 1)
                    f(std2[:, par], E_V[:, :], ACT.Sqrt, bias=eps[:, 0:1]).then_inc(std2_done, 1)
                if real(i - 2):
                    if since(i, 6):
                        act.wait_ge(wo_done, i - 4 - par)
                    for b in range(2):
                        act.wait_ge(l2_done, 2 * i - 3 + b)
                        for g in range(2 * b, 2 * b + 2):
                            src = E_H[first + b][:, (g % 2) * GC:(g % 2 + 1) * GC]
                            dst = hidF[:, ((k + 2) % 4) // 2].rearrange("p (j r) (b g v) -> p b g r j v", r=2, b=2, g=GROUPS)
                            last = f(dst[:, par, g], src.rearrange("p (r j v) -> p r j v", r=2, v=GV), ACT.Relu,
                                     bias=wuse[:, 1, par * GROUPS + g, HID:WE])
                        last.then_inc(hF_ready, 1)

            steps(act, 2, 4, route_experts, 2 * FRONT)

        @block.vector
        def _(dve):
            tt, stt, ts = nc.vector.tensor_tensor, nc.vector.scalar_tensor_tensor, nc.vector.tensor_scalar

            dve.wait_ge(tokw_in, 48)
            acc = rstd.rearrange("p a b -> p (a b)")[:, 0:2 * (HALF + 1) * D].rearrange(
                "p (s k o) -> p s k o", s=2, o=D)
            table = fold_table()
            for n in range(ROUNDS):
                if n:
                    dve.wait_ge(folded, n)
                for parity, (part, freq) in enumerate((EVEN[n], ODD[n])):
                    for k in range(HALF + 1):
                        if not table[:, n, parity, k].any():
                            continue
                        src, by_k = tokw_sb[:, 9 * part + freq], fold_sb[:, n, parity, k:k + 1]
                        if n == 0:
                            last = ts(acc[:, parity, k], src, by_k, None, ALU.mult)
                        else:
                            last = stt(acc[:, parity, k], src, by_k, acc[:, parity, k], ALU.mult, ALU.add)
                last.then_inc(folded, 1)
            dve.wait_ge(folded, ROUNDS)
            even_sum, odd_sum = acc[:, 0, 0:HALF], acc[:, 1, 0:HALF]
            tt(patch_w[:, :, 1], even_sum, odd_sum, ALU.add)
            tt(patch_w[:, :, 0], even_sum, odd_sum, ALU.subtract)
            tt(patch_w[:, :, 2], even_sum, odd_sum, ALU.subtract)
            tt(patch_end[:, 0:D], acc[:, 0, HALF - 1], acc[:, 1, HALF - 1], ALU.subtract)
            tt(patch_end[:, D:], acc[:, 0, HALF - 1], acc[:, 1, HALF - 1], ALU.add).then_inc(folded, 1)
            dve.wait_ge(folded, ROUNDS + 1)
            tt(patch_end[64:, D:], patch_end[64:, D:], acc[64:, 0, HALF], ALU.add).then_inc(folded, 1)
            dve.wait_ge(folded, ROUNDS + 2)
            tt(patch_end[64:, D:], patch_end[64:, D:], acc[64:, 1, HALF], ALU.add).then_inc(folded, 1)

            dve.wait_ge(route_in, 16)
            nc.vector.tensor_copy(route_f[:, 0], route_sb[:]).then_inc(route_step, 1)
            dve.wait_ge(route_step, 1)
            ts(route_f[:, 1], route_f[:, 0], 0.0, None, ALU.is_ge).then_inc(route_step, 1)
            ts(route_f[:, 2], route_f[:, 0], float(EXPERTS), -1.0, ALU.subtract, ALU.mult).then_inc(route_step, 1)
            dve.wait_ge(route_step, 3)
            stt(route_f[:, 3], route_f[:, 0], float(EXPERTS), route_f[:, 1], ALU.is_lt, ALU.mult).then_inc(route_step, 1)
            dve.wait_ge(route_step, 4)
            tt(route_f[:, 1], route_f[:, 2], route_f[:, 3], ALU.mult).then_inc(route_step, 1)
            dve.wait_ge(route_step, 5)
            ts(route_ix[:], route_f[:, 1], -1.0, float(EXPERTS), ALU.mult, ALU.add).then_inc(route_step, 1)

            dve.wait_ge(setup_pool, 1)

            def tokenize(i, k):
                other = 1 - k
                if real(i):
                    dve.wait_ge(odd_done, i + 1)
                    dve.wait_ge(odd_out, i + 1)
                    tt(cols(hT, i), P_ODD[k][:, :], odd_s[:, k], ALU.add).then_inc(added, 1)
                if real(i - 1):
                    dve.wait_ge(rooted, i)
                    if since(i, 3):
                        dve.wait_ge(normed, i - 2)
                    nc.vector.reciprocal(rstd[:, other], std[:, other]).then_inc(rstd_done, 1)
                    dve.wait_ge(rstd_done, i)
                    if since(i, 3):
                        dve.wait_ge(turned, i - 2)
                        dve.wait_ge(stored, i - 2)
                    tt(xh[:, other], P_C[other][:, :], rstd[:, other], ALU.mult).then_inc(normed, 1)

            steps(dve, 1, 2, tokenize)

            dve.wait_ge(alr_t, 1)
            ts(alr[:, :, 0], alr[:, :, 0], MAX_ALR / D / 2, MAX_ALR / D / 2, ALU.mult, ALU.add).then_inc(alr_done, 1)
            dve.wait_ge(alr_done, 1)

            def learn(i, k):
                other = 1 - k

                def turned_out_of(src, c, half):
                    return tt(dzt[:, half[0], :, half[1] * D:(half[1] + 1) * D], by(src[:, :], D),
                              alr[:, bass.ds(c * 2 * TILES, 2 * TILES), :].to_broadcast([128, 2 * TILES, D]), ALU.mult)

                def twice_derivative(s, c, made, done):
                    stt(c[:, k], s[:, k], 1.0, c[:, k], ALU.subtract, ALU.mult).then_inc(made, 1)
                    dve.wait_ge(made, i + 1)
                    return stt(c[:, k], s[:, k], 1.0, c[:, k], ALU.add, ALU.subtract).then_inc(done, 1)

                if real(i):
                    dve.wait_ge(t0_done, i + 1)
                    twice_derivative(s0, c0, m0_done, c0_done)
                if real(i - 1):
                    dve.wait_ge(back_done, i)
                    dve.wait_ge(dz1_done, i)
                    stt(dd[:, other], A_BACK[:, :], 0.5, dd[:, other], ALU.mult, ALU.add).then_inc(dy_done, 1)
                if real(i):
                    dve.wait_ge(t1_done, i + 1)
                    twice_derivative(s1, c1, m1_done, c1_done)
                    dve.wait_ge(d_done, i + 1)
                    dve.wait_ge(ss_done, i + 1)
                    tt(dd[:, k], A_D[:, :], dd[:, k], ALU.add).then_inc(dd_done, 1)
                    dve.wait_ge(dd_done, i + 1)
                    dve.wait_ge(c1_done, i + 1)
                    tt(c1[:, k], dd[:, k], c1[:, k], ALU.mult).then_inc(dz1_done, 1)
                if real(i - 2):
                    dve.wait_ge(dz0t_done, i - 1)
                    if since(i, 4):
                        dve.wait_ge(gw_done, i - 3)
                    turned_out_of(A_DZ0T, i - 2, (k, 0)).then_inc(dz0t_out, 1)
                if real(i - 1):
                    dve.wait_ge(dz1t_done, i)
                    if since(i, 3):
                        dve.wait_ge(gw_done, i - 2)
                    turned_out_of(A_DZ1T, i - 1, (other, 1)).then_inc(dz1t_out, 1)

            steps(dve, 2, 2, learn)

            old = W[:, AT["w0_dd"][0]:AT["b1_dd"][1]]
            dve.wait_ge(gw_done, B)
            nc.vector.tensor_copy(grad_s[:, :], A_G[:, 0:XW]).then_inc(learn_dve, 1)
            dve.wait_ge(learn_pe, 1)
            nc.vector.tensor_copy(gradt_s[:, :], A_Z0[:, 0:128]).then_inc(learn_dve, 1)
            dve.wait_ge(learn_pe, 2)
            g = A_Z1[:, 0:130]
            ts(adam[:, 0], g, -1.0, None, ALU.mult).then_inc(learn_dve, 1)
            dve.wait_ge(learn_dve, 3)
            tt(adam[:, 1], g, adam[:, 0], ALU.max).then_inc(learn_dve, 1)
            dve.wait_ge(learn_dve, 4)
            ts(adam[:, 1], adam[:, 1], ADAM_EPS, None, ALU.add).then_inc(learn_dve, 1)
            dve.wait_ge(learn_dve, 5)
            nc.vector.reciprocal(adam[:, 2], adam[:, 1]).then_inc(learn_dve, 1)
            dve.wait_ge(learn_dve, 6)
            stt(adam[:, 0], adam[:, 0], LR, adam[:, 2], ALU.mult, ALU.mult).then_inc(learn_dve, 1)
            dve.wait_ge(learn_dve, 7)
            stt(params[:, :], old, 1.0 - LR * WD, adam[:, 0], ALU.mult, ALU.add).then_inc(learn_dve, 1)
            dve.wait_ge(learn_dve, 8)
            for h in range(2):
                part, at_h = slice(64 * h, 64 * h + 64), slice(64 * h, 64 * h + 64)
                nc.vector.tensor_copy(n1_bd[part, at_h], params[part, 64:128]).then_inc(learn_dve, 1)
            dve.wait_ge(learn_pe, 3)
            for h in range(2):
                part, at_h = slice(64 * h, 64 * h + 64), slice(64 * h, 64 * h + 64)
                nc.vector.tensor_copy(r_w[part, :, at_h], by(A_D[part, 0:128], 64)).then_inc(learn_dve, 1)

            def retrieve(i, k):
                if real(i):
                    par = k % 2
                    dve.wait_ge(rq_done, i + 1)
                    dve.wait_ge(hs_done, i + 1)
                    tt(hs[:, par], R_Q[:, :], hs[:, par], ALU.add).then_inc(hq_done, 1)
                    dve.wait_ge(p1_done, i + 1)
                    dve.wait_ge(hq_done, i + 1)
                    if since(i, 4):
                        dve.wait_ge(h2t_done, i - 2 - par)
                        dve.wait_ge(h2_stored, i - 3)
                    tt(h2_of(k), by(hs[:, par], V), by(p1[:, par], V), ALU.add).then_inc(h2_done, 1)
                if k % 2 == 0 and since(i, 2):
                    for q in range(2):
                        dve.wait_ge(h2t_done, i - 1 + q)
                        tt(by(cols(resid, 2 * (i // 2) - 2 + q if isinstance(i, int) else i - 2 + q), D),
                           by(R_T[q][:, :], D),
                           w["bo"].rearrange("p (a n) -> p a n", a=1).to_broadcast([128, NJ, D]), ALU.add
                           ).then_inc(h2t_out, 1)

            steps(dve, 1, 4, retrieve)

            dve.wait_ge(h2_stored, B)
            dve.wait_ge(h2t_out, B)

            def route_experts(i, k):
                par = k % 2
                if real(i):
                    dve.wait_ge(std2_done, i + 1)
                    if since(i, 2):
                        dve.wait_ge(x2_done, i - 1)
                    nc.vector.reciprocal(rstd2[:, par], std2[:, par]).then_inc(rstd2_done, 1)
                    dve.wait_ge(rstd2_done, i + 1)
                    if since(i, 2):
                        dve.wait_ge(in_done, 2 * i - 2)
                    tt(x2[:, par], cols(hT, i), rstd2[:, par], ALU.mult).then_inc(x2_done, 1)
                if par == 0 and since(i, 4):
                    s = k // 2
                    if since(i, 8):
                        dve.wait_ge(out_dma[s], 4 * i - 16 - 8 * s)
                    for q in range(2):
                        dve.wait_ge(wo_done, i - 3 + q)
                        tt(outs[:, s, q * COLS:(q + 1) * COLS], E_O[q][:, :], cols(resid, i - 4 + q), ALU.add
                           ).then_inc(out_added, 1)

            steps(dve, 3, 4, route_experts, 2 * FRONT)

        @block.gpsimd
        def _(pool):
            tt, ts = nc.gpsimd.tensor_tensor, nc.gpsimd.tensor_scalar
            for buffer in (z_w, r_w, n1_bd, wi_p):
                last = nc.gpsimd.memset(buffer[:], 0.0)
            last.then_inc(zeroed, 1)
            nc.gpsimd.memset(eps[:], LN_EPS)
            nc.gpsimd.memset(odd_s[:, :, COLS - V:], 0.0)
            pool.wait_ge(w_in, 16)
            ts(half_b[:, 0:2], W[:, AT["b0_dd"][0]:AT["b1_dd"][1]], 0.5, 0.0, ALU.mult, ALU.add)
            ts(half_b[:, 2:3], w["blr"], 0.5, 0.0, ALU.mult, ALU.add)
            tt(d_w[:, :], w["wk_bd"], w["wv_bd"], ALU.subtract)
            for name in ("ws0", "ws1"):
                last = tt(w[name][:, 0:HID], w[name][:, 0:HID], w["ident"], ALU.add)
            last.then_inc(setup_pool, 1)
            nc.gpsimd.memset(rows3[:, :, 2 * D:], 1.0).then_inc(setup_pool, 1)

            def tokenize(i, k):
                if real(i):
                    pool.wait_ge(normed, i + 1)
                    nc.gpsimd.tensor_copy(cols(xT, i), xh[:, k]).then_inc(stored, 1)

            steps(pool, 0, 2, tokenize)

            def learn(i, k):
                other = 1 - k
                if real(i):
                    pool.wait_ge(s1_done, i + 1)
                    if since(i, 2):
                        pool.wait_ge(dz0_done, i - 1)
                    tt(dd[:, k], s0[:, k], s1[:, k], ALU.add).then_inc(ss_done, 1)
                if real(i - 1):
                    pool.wait_ge(dy_done, i)
                    pool.wait_ge(c0_done, i)
                    if since(i, 3):
                        pool.wait_ge(dz0t_done, i - 2)
                    tt(dz0[:, other], dd[:, other], c0[:, other], ALU.mult).then_inc(dz0_done, 1)

            steps(pool, 1, 2, learn)

            def retrieve(i, k):
                par = k % 2
                if real(i):
                    pool.wait_ge(p0_done, i + 1)
                    if since(i, 2):
                        pool.wait_ge(h2_done, i - 1)
                    tt(hs[:, par], cols(hT, i), p0[:, par], ALU.add).then_inc(hs_done, 1)
                if real(i - 1):
                    pool.wait_ge(stored, B)
                    pool.wait_ge(h2_done, i)
                    nc.gpsimd.tensor_copy(by(cols(hT, i - 1), V), h2_of((k - 1) % 4)).then_inc(h2_stored, 1)

            steps(pool, 1, 4, retrieve)

            pool.wait_ge(wr_in, 16)
            pool.wait_ge(route_step, 6)

            def route_experts(i, k):
                if real(i):
                    if since(i, 2):
                        pool.wait_ge(l2_done, 2 * i - 2)
                        pool.wait_ge(hF_ready, 2 * i - 2)
                    for g in range(GROUPS):
                        e = pool.value_load(route_ix[0:1, bass.ds(i * GROUPS + g, 1)], min_val=0, max_val=EXPERTS)
                        for l, name in enumerate(("ws0", "ws1")):
                            last = tt(wuse[:, l, k * GROUPS + g], wr[:, l, bass.ds(e, 1)].rearrange("p o n -> p (o n)"),
                                      w[name], ALU.add)
                    last.then_inc(wuse_ready, 1)

            steps(pool, 0, 2, route_experts)


def packed(inputs):
    def f(name):
        return np.asarray(inputs[name])

    eye, zero = np.eye(64, dtype=np.float32), np.zeros((64, 64), np.float32)

    def bd(a):
        return np.block([[a, zero], [zero, a]])

    def down(a):
        return np.concatenate([a, a], 0)

    wk, wq, wv, w1 = f("L0_attn_Wk"), f("L0_attn_Wq"), f("L0_attn_Wv"), f("L0_attn_Ws")[1]
    wlr = f("L0_attn_Wlr")
    ws, bs = f("L0_ffn_Ws"), f("L0_ffn_bs")
    third = np.full((64, 64), 1.0 / D, np.float32)
    parts = {
        "wk_bd": bd(wk), "wv_bd": bd(wv), "wq_bd": bd(wq), "w1_bd": bd(w1), "w1t_bd": bd(w1.T),
        "wkt_dd": np.block([[wk.T, wk.T], [zero, zero]]), "wqt_dd": np.block([[wq.T, wq.T], [zero, zero]]),
        "grad0": np.block([[wk, wk], [zero, zero]]), "grad1": np.block([[wk, wk], [eye, eye]]),
        "w0_dd": down(f("L0_attn_Ws")[0]), "w1_dd": down(w1),
        "b0_dd": down(f("L0_attn_bs")[0][:, None]), "b1_dd": down(f("L0_attn_bs")[1][:, None]),
        "wlr": np.block([[wlr, zero[:, :1]], [zero[:, :1], wlr]]),
        "blr": np.tile(f("L0_attn_blr")[None, :], (128, 1)),
        "wit_dd": down(f("L0_ffn_Wi").T), "bi": f("L0_ffn_bi")[:, None],
        "ws0": np.concatenate([ws[0, 0].T, bs[0, 0][:, None]], 1),
        "ws1": np.concatenate([ws[1, 0].T, bs[1, 0][:, None]], 1),
        "wot": f("L0_ffn_Wo").T, "bo": np.tile(f("L0_ffn_bo")[None, :], (128, 1)),
        "ident": np.eye(128, dtype=np.float32), "center": bd(eye - third), "mean": bd(third),
        "spread0": np.block([[eye, eye], [zero, zero]]), "spread1": np.block([[zero, zero], [eye, eye]]),
    }
    return np.ascontiguousarray(np.concatenate([parts[n] for n, _ in PACK], 1))


def kernel(**inputs):
    import concourse.bacc as bacc
    from concourse.bass_utils import run_bass_kernel_spmd

    tokw = np.asarray(inputs["L0_tok_W"]).reshape(D, 2, 9, C).transpose(3, 1, 2, 0).reshape(C, 18, D)
    wr, br = np.asarray(inputs["L0_ffn_Wr"]), np.asarray(inputs["L0_ffn_br"])
    experts = np.zeros((HID, LAYERS, EXPERTS + 1, WE), wr.dtype)
    experts[:, :, :EXPERTS, :HID] = wr.transpose(3, 0, 1, 2)
    experts[:, :, :EXPERTS, HID] = br.transpose(2, 0, 1)
    arrays = {
        "x": np.ascontiguousarray(inputs["x"]),
        "tokw": np.ascontiguousarray(tokw),
        "fold": fold_table(),
        "pack": packed(inputs),
        "experts": experts.reshape(HID, -1),
        "route": np.ascontiguousarray(inputs["L0_ffn_route_id"]).reshape(1, -1),
    }
    nc = bacc.Bacc("TRN2", target_bir_lowering=False, num_devices=1)
    args = [nc.dram_tensor(n, a.shape, mybir.dt.from_np(a.dtype), kind="ExternalInput").ap()
            for n, a in arrays.items()]
    out = nc.dram_tensor("out", (B, V * NP, D), F32, kind="ExternalOutput").ap()
    tower(nc, *args, out)
    r = run_bass_kernel_spmd(nc, [arrays], core_ids=[0])
    return r.results[0]["out"]
```

```python
from contextlib import ExitStack

import numpy as np

import concourse.bass as bass
from concourse import mybir

F32 = mybir.dt.float32
I32 = mybir.dt.int32
ALU = mybir.AluOpType
ACT = mybir.ActivationFunctionType
AX = mybir.AxisListType

B, C, T, V = 16, 64, 128, 64
D = 64
PATCH, STRIDE = 16, 8
NP = T // STRIDE
NJ = NP // 2
COLS = NJ * V
TILES = COLS // 128
HALF = STRIDE // 2
HID, EXPERTS, LAYERS = 128, 16, 2
GROUPS = 4
GV = V // GROUPS
GC = NP * GV
XW = 2 * D + 1
WE = HID + 1
LR, WD, MAX_ALR, ADAM_EPS, LN_EPS = 1e-3, 0.01, 0.1, 1e-8, 1e-5

PACK = [
    ("wk_bd", 128), ("wv_bd", 128), ("wq_bd", 128), ("w1_bd", 128), ("w1t_bd", 128),
    ("wkt_dd", 128), ("wqt_dd", 128), ("grad0", 128), ("grad1", 128),
    ("w0_dd", 64), ("w1_dd", 64), ("b0_dd", 1), ("b1_dd", 1),
    ("wlr_row", 64), ("blr", 1), ("wi0", 128), ("wi1", 128), ("bi", 1),
    ("ws0", WE), ("ws1", WE), ("wot", 64), ("bo", 64),
    ("ident", 128), ("spread0", 128), ("spread1", 128),
]
AT = {}
_at = 0
for _name, _w in PACK:
    AT[_name] = (_at, _at + _w)
    _at += _w
PACKED = _at

EVEN = [(0, f) for f in range(0, 9, 2)] + [(1, f) for f in range(2, 8, 2)]
ODD = [(0, f) for f in range(1, 9, 2)] + [(1, f) for f in range(1, 9, 2)]
ROUNDS = len(EVEN)
SUMS = 1 + ROUNDS.bit_length() - 1
TAIL_SUMS = SUMS + 1


def dft(part, f, k):
    a = 2 * np.pi * f * k / PATCH
    return (np.cos(a) if part == 0 else -np.sin(a)) / np.sqrt(PATCH)


def fold_table():
    t = np.zeros((128, ROUNDS, 2, HALF + 1))
    for n in range(ROUNDS):
        for parity, (part, f) in enumerate((EVEN[n], ODD[n])):
            for h in range(2):
                for k in range(HALF):
                    t[64 * h:64 * h + 64, n, parity, k] = dft(part, f, HALF * h + k)
            t[:, n, parity, HALF] = sum(dft(part, f, k) for k in range(STRIDE, PATCH))
    t[abs(t) < 1e-12] = 0.0
    return t.astype(np.float32).reshape(128, -1)


FRONT = 4


def steps(eng, lag, unroll, step, front=FRONT, done=0):
    for i in range(done, front):
        step(i, i % unroll)
    with eng.Fori(0, (B - front) // unroll) as n:
        for k in range(unroll):
            step(n * unroll + front + k, (front + k) % unroll)
    for i in range(B, B + lag):
        step(i, i % unroll)


def real(c, n=B):
    return not isinstance(c, int) or 0 <= c < n


def since(c, first):
    return not isinstance(c, int) or c >= first


def tower(nc, x, tokw, pack, experts, route, out):
    ctx = ExitStack()
    with ctx:
        def sb(name, shape, dt=F32):
            return ctx.enter_context(nc.sbuf_tensor(name, shape, dt))

        def sem(name):
            return ctx.enter_context(nc.semaphore(name))

        hT = sb("hT", [128, B * COLS])
        xT = sb("xT", [128, B * COLS])
        rows = sb("rows", [128, B * TILES * 2 * XW])
        W = sb("W", [128, PACKED])
        w = {n: W[:, a:b] for n, (a, b) in AT.items()}
        tokw_sb = xT[:, 0:2 * ROUNDS * (D + HALF + 1)]
        freq_w = tokw_sb[:, 0:2 * ROUNDS * D].rearrange("p (f a o) -> p f a o", a=1, o=D)
        coef = tokw_sb[:, 2 * ROUNDS * D:].rearrange("p (f k a) -> p f k a", k=HALF + 1, a=1)
        p_at = tokw_sb.shape[1]
        terms = xT[:, p_at:p_at + 2 * ROUNDS * HALF * D].rearrange("p (n s k o) -> p n s k o", n=ROUNDS, s=2, o=D)
        t_at = p_at + 2 * ROUNDS * HALF * D
        tails = xT[:, t_at:t_at + 2 * ROUNDS * D].rearrange("p (f o) -> p f o", o=D)
        patch_w = sb("patch_w", [128, HALF, 3, D])
        patch_end = sb("patch_end", [128, 2 * D])
        z_w = sb("z_w", [128, 2, 128])
        d_w = sb("d_w", [128, 128])
        r_w = sb("r_w", [128, 128])
        n1_bd = sb("n1_bd", [128, 128])
        logit = sb("logit", [128, B * TILES * 2])
        alr = sb("alr", [128, B * TILES * 2, 1])
        half_b = sb("half_b", [128, 3])
        eps = sb("eps", [128, 1])
        stats = sb("stats", [128, 4, 2, NP])
        grad_s = sb("grad_s", [128, XW])
        gradt_s = sb("gradt_s", [128, 128])
        adam = sb("adam", [128, 3, 130])
        params = sb("params", [128, 130])
        route_sb = sb("route_sb", [1, B * GROUPS], I32)
        route_f = sb("route_f", [1, 4, B * GROUPS])
        route_ix = sb("route_ix", [1, B * GROUPS], I32)

        arena = sb("arena", [128, 14 * 1024])
        at = [0]

        def scratch(*shape):
            n = int(np.prod(shape))
            a = arena[:, at[0]:at[0] + n]
            at[0] += n
            if len(shape) == 2:
                return a.rearrange("p (a b) -> p a b", b=shape[1])
            if len(shape) == 3:
                return a.rearrange("p (a b c) -> p a b c", b=shape[1], c=shape[2])
            return a

        xb = scratch(2, 2 * NJ, HALF * V)
        odd_s = scratch(2, COLS)
        h_new, cen, sq, xh, xlr = (scratch(2, COLS) for _ in range(5))
        at[0] = 0
        s0, c0, s1, c1, dd, dz0 = (scratch(2, COLS) for _ in range(6))
        dzt = scratch(2, 2 * TILES, 2 * D)
        at[0] = 0
        p0, p1, hs, y1 = (scratch(2, COLS) for _ in range(4))
        h2 = scratch(2, NJ, 2 * V)
        at[0] = 0
        x2 = scratch(2, NJ, 2 * V)
        outs = scratch(2, NP * D)
        hid0, hid1 = (scratch(NP * V) for _ in range(2))
        cen2, sq2, xh2 = (scratch(NP, D) for _ in range(3))
        hidF = scratch(2, NP, 2 * V)
        resid = rows[:, 0:B // 2 * NP * D]
        e0 = B // 2 * NP * D
        e1 = e0 + LAYERS * (EXPERTS + 1) * WE
        wr = rows[:, e0:e1].rearrange("p (l e n) -> p l e n", l=LAYERS, n=WE)
        e2 = e1 + LAYERS * 2 * GROUPS * WE
        assert e2 <= B * TILES * 2 * XW
        wuse = rows[:, e1:e2].rearrange("p (l s n) -> p l s n", l=LAYERS, n=WE)
        rows3 = rows[:, :].rearrange("p (t n) -> p t n", n=XW)

        bank = [ctx.enter_context(nc.psum_tensor(f"bank{n}", [128, COLS], F32)) for n in range(8)]

        def by(ap, n):
            return ap.rearrange("p (a n) -> p a n", n=n)

        x_in = [sem("x_in0"), sem("x_in1")]
        w_in, tokw_in, wr_in, route_in = sem("w_in"), sem("tokw_in"), sem("wr_in"), sem("route_in")
        zeroed, folded, setup_pe, setup_act, setup_pool = (
            sem(n) for n in ("zeroed", "folded", "setup_pe", "setup_act", "setup_pool"))
        odd_done, even_done, odd_out, added, turned, summed, centred, squared = (
            sem(n) for n in ("odd_done", "even_done", "odd_out", "added", "turned", "summed",
                             "centred", "squared"))
        sq_summed, rooted, rate_done, normed, in_rows, xlr_done, logit_done, back_turned, stored = (
            sem(n) for n in ("sq_summed", "rooted", "rate_done", "normed", "in_rows", "xlr_done",
                             "logit_done", "back_turned", "stored"))
        kept = sem("kept")
        alr_t, alr_done, tail_done = sem("alr_t"), sem("alr_done"), sem("tail_done")
        z0_done, d_done, z1_done, s0_done, t0_done, s1_done, t1_done = (
            sem(n) for n in ("z0_done", "d_done", "z1_done", "s0_done", "t0_done", "s1_done", "t1_done"))
        m0_done, c0_done, m1_done, c1_done, ss_done, dd_done, dz1_done = (
            sem(n) for n in ("m0_done", "c0_done", "m1_done", "c1_done", "ss_done", "dd_done", "dz1_done"))
        back_done, dy_done, dz0_done, s0t_done, s0t_out, dz1t_done, dz1t_out, dz0t_done, dz0t_out = (
            sem(n) for n in ("back_done", "dy_done", "dz0_done", "s0t_done", "s0t_out", "dz1t_done",
                             "dz1t_out", "dz0t_done", "dz0t_out"))
        gw_done, learn_pe, learn_dve = sem("gw_done"), sem("learn_pe"), sem("learn_dve")
        rz0_done, rq_done, rz1_done, p0_done, p1_done, hs_done, y1_done, h2_done = (
            sem(n) for n in ("rz0_done", "rq_done", "rz1_done", "p0_done", "p1_done", "hs_done",
                             "y1_done", "h2_done"))
        h2t_done, h2t_out = sem("h2t_done"), sem("h2t_out")
        summed2, centred2, squared2, sq_summed2, rooted2, rate2_done, normed2, turned2, biased = (
            sem(n) for n in ("summed2", "centred2", "squared2", "sq_summed2", "rooted2", "rate2_done",
                             "normed2", "turned2", "biased"))
        x2_done = sem("x2_done")
        in_done, l1_done, l2_done, h0_ready, h1_ready, hF_ready = (
            sem(n) for n in ("in_done", "l1_done", "l2_done", "h0_ready", "h1_ready", "hF_ready"))
        wo_done, out_added, wuse_ready, route_step = (
            sem(n) for n in ("wo_done", "out_added", "wuse_ready", "route_step"))
        out_dma = [sem("out_dma0"), sem("out_dma1")]

        P_ODD, P_EVEN, P_H, P_X, P_W = bank[0:2], bank[2], bank[3], bank[5], bank[7]
        A_Z0, A_Z1, A_D, A_BACK, A_S0T, A_DZ1T, A_DZ0T, A_G = bank
        R_Z0, R_Q, R_Z1, R_T = bank[0:2], bank[2:4], bank[4], bank[5:7]
        E_O, E_X, E_H = bank[0:2], bank[2:4], bank[4:8]

        xs = x.rearrange("b c (m h t) v -> b h c m (t v)", h=2, t=HALF)
        out_rows = out.rearrange("b (v n) d -> (b v) (n d)", n=NP)

        def cols(tensor, c, n=COLS):
            return tensor[:, bass.ds(c * n, n)]

        def h2_of(k):
            return h2[:, k // 2].rearrange("p j (b v) -> p b j v", b=2)[:, k % 2]

        block = ctx.enter_context(nc.Block())

        @block.sync
        def _(sp):
            def load_x(i, k):
                if since(i, 2):
                    sp.wait_ge(even_done, i - 1)
                for h in range(2):
                    sp.dma_start(xb[64 * h:64 * h + 64, k], xs[bass.ds(i, 1), h].rearrange("o c m n -> c (o m) n")
                                 ).then_inc(x_in[k], 16)

            sp.dma_start(tokw_sb, tokw).then_inc(tokw_in, 16)
            load_x(0, 0)
            sp.dma_start(W[:, :], pack).then_inc(w_in, 16)
            load_x(1, 1)
            sp.dma_start(route_sb[:], route).then_inc(route_in, 16)
            with sp.Fori(1, B // 2) as n:
                for k in range(2):
                    load_x(2 * n + k, k)
            sp.wait_ge(gw_done, B)
            sp.dma_start(rows[:, e0:e1], experts).then_inc(wr_in, 16)

            def store(p, s, row):
                sp.wait_ge(out_added, 2 * p + 2)
                sp.dma_start(out_rows[bass.ds(row, 128), :], outs[:, s]).then_inc(out_dma[s], 16)

            with sp.Fori(0, B // 4) as n:
                for s in range(2):
                    store(2 * n + s, s, n * 256 + s * 128)
            for s in range(2):
                sp.wait_ge(out_dma[s], 16 * (B // 4))

        @block.tensor
        def _(pe):
            mm, tr = nc.tensor.matmul, nc.tensor.transpose

            pe.wait_ge(w_in, 16)
            mm(P_W[:, 0:64], w["wkt_dd"][0:64], w["w0_dd"][0:64], start=True, stop=True)
            mm(P_W[:, 64:128], w["wkt_dd"][0:64], w["w1_dd"][0:64], start=True, stop=True).then_inc(setup_pe, 1)

            pe.wait_ge(folded, SUMS + 2)

            def tokenize(i, k):
                k = k % 2
                if real(i):
                    pe.wait_ge(x_in[k], 16 * (i - k) + 32)
                    if since(i, 2):
                        pe.wait_ge(added, i - 1)
                    xm = xb[:, k].rearrange("p (j o) (t v) -> p j o t v", o=2, t=HALF)
                    for t in (0, HALF - 1, *range(1, HALF - 1)):
                        lhs = patch_w[:, t, 0:2].rearrange("p a b -> p (a b)")
                        if t < HALF - 1:
                            last = mm(P_ODD[k][:, :], lhs, xm[:, :, 1, t], start=(t == 0), stop=(t == HALF - 2))
                        else:
                            mm(P_ODD[k][:, 0:COLS - V], lhs, xm[:, 0:NJ - 1, 1, t], start=False, stop=False,
                               skip_group_check=True)
                            mm(P_ODD[k][:, COLS - V:], patch_end[:, :], xm[:, NJ - 1, 1, t], start=False,
                               stop=False, skip_group_check=True)
                    last.then_inc(odd_done, 1)
                if real(i - 1):
                    pe.wait_ge(added, i)
                    if since(i, 2):
                        pe.wait_ge(centred, i - 1)
                    for t in range(TILES):
                        last = tr(P_H[:, 128 * t:128 * t + 128], h_new[:, 1 - k, 128 * t:128 * t + 128], w["ident"])
                    last.then_inc(turned, 1)
                if real(i - 2):
                    pe.wait_ge(normed, i - 1)
                    if since(i, 3):
                        pe.wait_ge(stored, i - 2)
                    for t in range(TILES):
                        last = tr(P_X[:, 128 * t:128 * t + 128], xh[:, k, 128 * t:128 * t + 128], w["ident"])
                    last.then_inc(back_turned, 1)
                if real(i):
                    if since(i, 1):
                        pe.wait_ge(odd_out, i)
                    for t in range(HALF):
                        last = mm(P_EVEN[:, :], patch_w[:, t, 1:3].rearrange("p a b -> p (a b)"),
                                  xm[:, :, 0, t], start=(t == 0), stop=(t == HALF - 1))
                    last.then_inc(even_done, 1)

            steps(pe, 1, 2, tokenize)

            pe.wait_ge(added, B)
            pe.wait_ge(setup_pool, 1)

            def learn(i, k):
                other = 1 - k
                if real(i):
                    pe.wait_ge(stored, i + 1)
                    if since(i, 1):
                        pe.wait_ge(t0_done, i)
                    mm(A_Z0[:, :], z_w[:, 0], cols(xT, i), start=True, stop=True).then_inc(z0_done, 1)
                if real(i - 1):
                    if since(i, 2):
                        pe.wait_ge(s0t_out, i - 1)
                    for t in range(TILES):
                        tile = slice(128 * t, 128 * t + 128)
                        last = tr(A_S0T[:, tile], s0[:, other, tile], w["ident"])
                    last.then_inc(s0t_done, 1)
                if real(i):
                    if since(i, 1):
                        pe.wait_ge(dd_done, i)
                    mm(A_D[:, :], d_w[:, :], cols(xT, i), start=True, stop=True).then_inc(d_done, 1)
                if real(i - 2):
                    pe.wait_ge(dz0_done, i - 1)
                    if since(i, 3):
                        pe.wait_ge(dz0t_out, i - 2)
                    for t in range(TILES):
                        tile = slice(128 * t, 128 * t + 128)
                        last = tr(A_DZ0T[:, tile], dz0[:, k, tile], w["ident"])
                    last.then_inc(dz0t_done, 1)
                if real(i):
                    if since(i, 1):
                        pe.wait_ge(t1_done, i)
                    mm(A_Z1[:, :], z_w[:, 1], cols(xT, i), start=True, stop=False)
                    pe.wait_ge(s0_done, i + 1)
                    mm(A_Z1[:, :], w["w1_bd"], s0[:, k], start=False, stop=True).then_inc(z1_done, 1)
                if real(i - 2):
                    pe.wait_ge(s0t_out, i - 1)
                    pe.wait_ge(dz0t_out, i - 1)
                    pe.wait_ge(dz1t_out, i - 1)
                    for t in range(2 * TILES):
                        first = isinstance(i, int) and i == 2 and t == 0
                        final = isinstance(i, int) and i == B + 1 and t == 2 * TILES - 1
                        last = mm(A_G[:, 0:XW], dzt[:, k, t], cols(rows, (i - 2) * 2 * TILES + t, XW),
                                  start=first, stop=final, skip_group_check=True)
                    last.then_inc(gw_done, 1)
                if real(i - 1):
                    pe.wait_ge(dz1_done, i)
                    if since(i, 2):
                        pe.wait_ge(dy_done, i - 1)
                    mm(A_BACK[:, :], w["w1t_bd"], c1[:, other], start=True, stop=True).then_inc(back_done, 1)
                    if since(i, 2):
                        pe.wait_ge(dz1t_out, i - 1)
                    for t in range(TILES):
                        tile = slice(128 * t, 128 * t + 128)
                        last = tr(A_DZ1T[:, tile], c1[:, other, tile], w["ident"])
                    last.then_inc(dz1t_done, 1)

            for i in range(2):
                learn(i, i)
                if i == 0:
                    tokenize(B + 1, 1)
                    pe.wait_ge(stored, B)
                    pe.wait_ge(setup_act, 1)
            steps(pe, 2, 2, learn, done=2)

            pe.wait_ge(learn_dve, 1)
            tr(A_Z0[:, 0:128], grad_s[:, 0:128], w["ident"]).then_inc(learn_pe, 1)
            mm(A_Z1[:, 128:129], w["spread0"], grad_s[:, 128:129], start=True, stop=True)
            mm(A_Z1[:, 129:130], w["spread1"], grad_s[:, 128:129], start=True, stop=True)
            pe.wait_ge(learn_dve, 2)
            mm(A_Z1[:, 0:64], w["grad0"], gradt_s[:, 0:64], start=True, stop=True)
            mm(A_Z1[:, 64:128], w["grad1"], gradt_s[:, 64:128], start=True, stop=True).then_inc(learn_pe, 1)
            pe.wait_ge(learn_dve, 8)
            mm(A_D[:, 0:D], w["wqt_dd"][0:64], params[0:64, 0:D], start=True, stop=True).then_inc(learn_pe, 1)
            pe.wait_ge(learn_dve, 12)

            def retrieve(i, k):
                other = 1 - k % 2
                if real(i):
                    if since(i, 2):
                        pe.wait_ge(p0_done, i - 1)
                    mm(R_Z0[k % 2][:, :], r_w[:, :], cols(xT, i), start=True, stop=True).then_inc(rz0_done, 1)
                    if since(i, 2):
                        pe.wait_ge(y1_done, i - 1)
                    mm(R_Q[k % 2][:, :], w["wq_bd"], cols(xT, i), start=True, stop=True).then_inc(rq_done, 1)
                if real(i - 1):
                    pe.wait_ge(y1_done, i)
                    if since(i, 2):
                        pe.wait_ge(p1_done, i - 1)
                    mm(R_Z1[:, :], n1_bd[:, :], y1[:, other], start=True, stop=True).then_inc(rz1_done, 1)
                if k % 2 == 1 and since(i, 3):
                    pe.wait_ge(h2_done, i - 1)
                    if since(i, 5):
                        pe.wait_ge(h2t_out, i - 3)
                    pair = ((k - 3) % 4) // 2
                    for q in range(2):
                        for j in range(NJ // 2):
                            last = tr(R_T[q][:, 128 * j:128 * j + 128], h2[:, pair, q * NJ // 2 + j], w["ident"])
                        last.then_inc(h2t_done, 1)

            steps(pe, 2, 4, retrieve)

            pe.wait_ge(h2t_out, B)

            def route_experts(i, k):
                par = k % 2
                first, second = 2 * par, 2 * (1 - par)
                if real(i - 2):
                    pe.wait_ge(x2_done, i - par)
                    if since(i, 3):
                        pe.wait_ge(h1_ready, 2 * i - 4)
                    xv = x2[:, (k + 2) % 4 // 2].rearrange("p j (b g v) -> p b g j v", b=2, v=GV)[:, par]
                    for b in range(2):
                        hv = E_H[first + b][:, :].rearrange("p (g r j v) -> p r g j v", g=2, r=2, v=GV)
                        for r in range(2):
                            last = mm(hv[:, r], w[f"wi{r}"], xv[:, 2 * b:2 * b + 2], start=True, stop=True)
                        last.then_inc(in_done, 1)
                if par == 1 and real(i):
                    pe.wait_ge(normed2, (i + 1) // 2)
                    if since(i, 3):
                        pe.wait_ge(x2_done, i - 1)
                    for j in range(NJ):
                        tile = xh2[:, 2 * j:2 * j + 2].rearrange("p a b -> p (a b)")
                        last = tr(E_X[j // 4][:, j % 4 * 128:(j % 4 + 1) * 128], tile, w["ident"])
                        if j % 4 == 3:
                            last.then_inc(turned2, 1)
                if since(i, 4):
                    if par == 0:
                        pe.wait_ge(hF_ready, 2 * i - 4)
                    if since(i, 6):
                        pe.wait_ge(out_added, i - 5)
                    for n in range(NJ):
                        last = mm(E_O[par][:, n * D:(n + 1) * D], hidF[:, (k - par) // 2, NJ * par + n], w["wot"],
                                  start=True, stop=True)
                    last.then_inc(wo_done, 1)
                if real(i - 2):
                    pe.wait_ge(wuse_ready, i - 1)
                    if since(i, 3):
                        pe.wait_ge(hF_ready, 2 * i - 4)
                    for b in range(2):
                        pe.wait_ge(h0_ready, 2 * i - 3 + b)
                        for g in range(2 * b, 2 * b + 2):
                            last = mm(E_H[second + b][:, (g % 2) * GC:(g % 2 + 1) * GC], wuse[:, 0, par * GROUPS + g, 0:HID],
                                      hid0[:, g * GC:(g + 1) * GC], start=True, stop=True)
                        last.then_inc(l1_done, 1)
                if real(i - 2):
                    for b in range(2):
                        pe.wait_ge(h1_ready, 2 * i - 3 + b)
                        for g in range(2 * b, 2 * b + 2):
                            last = mm(E_H[first + b][:, (g % 2) * GC:(g % 2 + 1) * GC], wuse[:, 1, par * GROUPS + g, 0:HID],
                                      hid1[:, g * GC:(g + 1) * GC], start=True, stop=True)
                        last.then_inc(l2_done, 1)

            steps(pe, 4, 4, route_experts, 2 * FRONT)

        @block.scalar
        def _(act):
            f = nc.scalar.activation

            act.wait_ge(setup_pe, 1)
            act.wait_ge(zeroed, 1)
            for h in range(2):
                part = slice(64 * h, 64 * h + 64)
                last = f(z_w[part, :, 64 * h:64 * h + 64], by(P_W[part, 0:128], 64), ACT.Copy)
            last.then_inc(setup_act, 1)

            def tokenize(i, k):
                other = 1 - k
                if real(i - 1):
                    act.wait_ge(centred, i)
                    if since(i, 3):
                        act.wait_ge(sq_summed, i - 2)
                    f(sq[:, other], cen[:, other], ACT.Square).then_inc(squared, 1)
                if real(i - 2):
                    act.wait_ge(back_turned, i - 1)
                    f(cols(xT, i - 2), P_X[:, :], ACT.Copy).then_inc(stored, 1)
                if real(i - 1):
                    act.wait_ge(sq_summed, i)
                    f(stats[:, 2, other, 0:NJ], stats[:, 1, other, 0:NJ], ACT.Sqrt, bias=eps[:, 0:1], scale=1 / D
                      ).then_inc(rooted, 1)
                if real(i - 2):
                    act.wait_ge(normed, i - 1)
                    f(rows3[:, bass.ds((i - 2) * 2 * TILES, 2 * TILES), 0:D], by(xh[:, k], D), ACT.Copy
                      ).then_inc(in_rows, 1)
                if real(i):
                    act.wait_ge(even_done, i + 1)
                    if since(i, 2):
                        act.wait_ge(added, i - 1)
                    f(odd_s[0:64, k], P_EVEN[0:64, :], ACT.Copy)
                    f(odd_s[64:128, k, 0:COLS - V], P_EVEN[64:128, V:], ACT.Copy).then_inc(odd_out, 1)

            act.wait_ge(setup_pool, 1)
            steps(act, 1, 2, tokenize)

            def learn(i, k):
                other = 1 - k
                if real(i):
                    act.wait_ge(z0_done, i + 1)
                    if since(i, 2):
                        act.wait_ge(s0t_done, i - 1)
                        act.wait_ge(z1_done, i - 1)
                        act.wait_ge(c0_done, i - 1)
                        act.wait_ge(dz0_done, i - 1)
                        act.wait_ge(ss_done, i - 1)
                    f(s0[:, k], A_Z0[:, :], ACT.Silu, bias=w["b0_dd"]).then_inc(s0_done, 1)
                    f(c0[:, k], A_Z0[:, :], ACT.Tanh, bias=half_b[:, 0:1], scale=0.5).then_inc(t0_done, 1)
                if real(i - 1):
                    act.wait_ge(s0t_done, i)
                    f(rows3[:, bass.ds((i - 1) * 2 * TILES, 2 * TILES), D:2 * D], by(A_S0T[:, :], D), ACT.Copy
                      ).then_inc(s0t_out, 1)
                if real(i):
                    act.wait_ge(z1_done, i + 1)
                    if since(i, 2):
                        act.wait_ge(c1_done, i - 1)
                        act.wait_ge(dz1t_done, i - 1)
                    f(s1[:, k], A_Z1[:, :], ACT.Silu, bias=w["b1_dd"]).then_inc(s1_done, 1)
                    f(c1[:, k], A_Z1[:, :], ACT.Tanh, bias=half_b[:, 1:2], scale=0.5).then_inc(t1_done, 1)

            learn(0, 0)
            tokenize(B + 1, 1)
            act.wait_ge(logit_done, B)
            f(alr[:, :, 0], logit[:, :], ACT.Tanh, bias=half_b[:, 2:3], scale=0.5).then_inc(alr_t, 1)
            steps(act, 1, 2, learn, done=1)

            def retrieve(i, k):
                other = 1 - k
                if real(i):
                    act.wait_ge(rz0_done, i + 1)
                    if since(i, 2):
                        act.wait_ge(y1_done, i - 1)
                    f(p0[:, k], R_Z0[k][:, :], ACT.Silu, bias=params[:, 128:129]).then_inc(p0_done, 1)
                if real(i - 1):
                    act.wait_ge(rz1_done, i)
                    if since(i, 3):
                        act.wait_ge(hs_done, i - 2)
                    f(p1[:, other], R_Z1[:, :], ACT.Silu, bias=params[:, 129:130]).then_inc(p1_done, 1)

            steps(act, 1, 2, retrieve)

            act.wait_ge(h2t_done, B)

            def route_experts(i, k):
                par = k % 2
                first, second = 2 * par, 2 * (1 - par)
                if real(i - 2):
                    if since(i, 3):
                        act.wait_ge(l1_done, 2 * i - 4)
                    for b in range(2):
                        act.wait_ge(in_done, 2 * i - 3 + b)
                        f(hid0[:, b * COLS:(b + 1) * COLS], E_H[first + b][:, :], ACT.Relu, bias=w["bi"]
                          ).then_inc(h0_ready, 1)
                if par == 0 and real(i):
                    act.wait_ge(centred2, i // 2 + 1)
                    if since(i, 2):
                        act.wait_ge(sq_summed2, i // 2)
                    f(sq2, cen2, ACT.Square).then_inc(squared2, 1)
                if real(i - 2):
                    if since(i, 3):
                        act.wait_ge(l2_done, 2 * i - 4)
                    for b in range(2):
                        act.wait_ge(l1_done, 2 * i - 3 + b)
                        for g in range(2 * b, 2 * b + 2):
                            last = f(hid1[:, g * GC:(g + 1) * GC], E_H[second + b][:, (g % 2) * GC:(g % 2 + 1) * GC],
                                     ACT.Relu, bias=wuse[:, 0, par * GROUPS + g, HID:WE])
                        last.then_inc(h1_ready, 1)
                if par == 0 and real(i):
                    act.wait_ge(sq_summed2, i // 2 + 1)
                    f(stats[:, 2, 0], stats[:, 1, 0], ACT.Sqrt, bias=eps[:, 0:1], scale=1 / D).then_inc(rooted2, 1)
                if par == 1 and real(i):
                    for q in range(2):
                        act.wait_ge(turned2, i + q)
                        if since(i, 5):
                            act.wait_ge(in_done, 2 * i - 6)
                        f(x2[:, k // 2, q * NJ // 2:(q + 1) * NJ // 2].rearrange("p a b -> p (a b)"), E_X[q][:, :],
                          ACT.Copy).then_inc(x2_done, 1)
                if real(i - 2):
                    if since(i, 6):
                        act.wait_ge(wo_done, i - 4 - par)
                    for b in range(2):
                        act.wait_ge(l2_done, 2 * i - 3 + b)
                        for g in range(2 * b, 2 * b + 2):
                            src = E_H[first + b][:, (g % 2) * GC:(g % 2 + 1) * GC]
                            dst = hidF[:, ((k + 2) % 4) // 2].rearrange("p (j r) (b g v) -> p b g r j v", r=2, b=2, g=GROUPS)
                            last = f(dst[:, par, g], src.rearrange("p (r j v) -> p r j v", r=2, v=GV), ACT.Relu,
                                     bias=wuse[:, 1, par * GROUPS + g, HID:WE])
                        last.then_inc(hF_ready, 1)

            steps(act, 2, 4, route_experts, 2 * FRONT)

        @block.vector
        def _(dve):
            tt, stt, ts = nc.vector.tensor_tensor, nc.vector.scalar_tensor_tensor, nc.vector.tensor_scalar
            reduce = nc.vector.tensor_reduce

            def each(a):
                return a.rearrange("p (n o) -> p n o", o=1).to_broadcast([128, a.shape[1], D])


            dve.wait_ge(tokw_in, 16)
            wide = [128, 2 * ROUNDS, HALF, D]
            tt(terms.rearrange("p n s k o -> p (n s) k o"), freq_w.to_broadcast(wide),
               coef[:, :, 0:HALF].to_broadcast(wide), ALU.mult).then_inc(folded, 1)
            n = ROUNDS // 2
            while n:
                dve.wait_ge(folded, 1 + (ROUNDS // 2 // n).bit_length() - 1)
                tt(terms[:, 0:n], terms[:, 0:n], terms[:, n:2 * n], ALU.add).then_inc(folded, 1)
                n //= 2
            dve.wait_ge(folded, SUMS)
            even_sum, odd_sum = terms[:, 0, 0], terms[:, 0, 1]
            tt(patch_w[:, :, 1], even_sum, odd_sum, ALU.add)
            tt(patch_w[:, :, 0], even_sum, odd_sum, ALU.subtract)
            tt(patch_end[:, 0:D], even_sum[:, HALF - 1], odd_sum[:, HALF - 1], ALU.subtract)
            tt(patch_end[:, D:], even_sum[:, HALF - 1], odd_sum[:, HALF - 1], ALU.add).then_inc(folded, 1)
            tt(patch_w[:, :, 2], even_sum, odd_sum, ALU.subtract)
            dve.wait_ge(folded, SUMS + 1)
            dve.wait_ge(tail_done, TAIL_SUMS)
            tt(patch_end[64:, D:], patch_end[64:, D:], tails[64:, 0], ALU.add).then_inc(folded, 1)

            dve.wait_ge(route_in, 16)
            nc.vector.tensor_copy(route_f[:, 0], route_sb[:]).then_inc(route_step, 1)
            dve.wait_ge(route_step, 1)
            ts(route_f[:, 1], route_f[:, 0], 0.0, None, ALU.is_ge).then_inc(route_step, 1)
            ts(route_f[:, 2], route_f[:, 0], float(EXPERTS), -1.0, ALU.subtract, ALU.mult).then_inc(route_step, 1)
            dve.wait_ge(route_step, 3)
            stt(route_f[:, 3], route_f[:, 0], float(EXPERTS), route_f[:, 1], ALU.is_lt, ALU.mult).then_inc(route_step, 1)
            dve.wait_ge(route_step, 4)
            tt(route_f[:, 1], route_f[:, 2], route_f[:, 3], ALU.mult).then_inc(route_step, 1)
            dve.wait_ge(route_step, 5)
            ts(route_ix[:], route_f[:, 1], -1.0, float(EXPERTS), ALU.mult, ALU.add).then_inc(route_step, 1)

            dve.wait_ge(setup_pool, 1)

            def tokenize(i, k):
                other = 1 - k
                if real(i - 1):
                    total, sq_total, root, rate = (stats[:, n, other, 0:NJ] for n in range(4))
                    tokens = by(P_H[:, :], D)
                    dve.wait_ge(turned, i)
                    if since(i, 3):
                        dve.wait_ge(centred, i - 2)
                    reduce(total, tokens, AX.X, ALU.add).then_inc(summed, 1)
                    dve.wait_ge(summed, i)
                    if since(i, 3):
                        dve.wait_ge(squared, i - 2)
                        dve.wait_ge(normed, i - 2)
                    stt(by(cen[:, other], D), each(total), -1 / D, tokens, ALU.mult, ALU.add).then_inc(centred, 1)
                if real(i - 2):
                    dve.wait_ge(xlr_done, i - 1)
                    reduce(cols(logit, i - 2, 2 * TILES), by(xlr[:, k], D), AX.X, ALU.add).then_inc(logit_done, 1)
                if real(i - 1):
                    dve.wait_ge(squared, i)
                    if since(i, 3):
                        dve.wait_ge(rooted, i - 2)
                    reduce(sq_total, by(sq[:, other], D), AX.X, ALU.add).then_inc(sq_summed, 1)
                    dve.wait_ge(rooted, i)
                    if since(i, 3):
                        dve.wait_ge(normed, i - 2)
                    nc.vector.reciprocal(rate, root).then_inc(rate_done, 1)
                    dve.wait_ge(rate_done, i)
                    dve.wait_ge(centred, i)
                    if since(i, 3):
                        dve.wait_ge(back_turned, i - 2)
                        dve.wait_ge(in_rows, i - 2)
                        dve.wait_ge(xlr_done, i - 2)
                    tt(by(xh[:, other], D), by(cen[:, other], D), each(rate), ALU.mult).then_inc(normed, 1)
                if real(i):
                    dve.wait_ge(odd_done, i + 1)
                    dve.wait_ge(odd_out, i + 1)
                    if since(i, 2):
                        dve.wait_ge(turned, i - 1)
                        dve.wait_ge(kept, i - 1)
                    tt(h_new[:, k], P_ODD[k][:, :], odd_s[:, k], ALU.add).then_inc(added, 1)

            steps(dve, 2, 2, tokenize)


            def learn(i, k):
                other = 1 - k

                def turned_out_of(src, c, half):
                    return tt(dzt[:, half[0], :, half[1] * D:(half[1] + 1) * D], by(src[:, :], D),
                              alr[:, bass.ds(c * 2 * TILES, 2 * TILES), :].to_broadcast([128, 2 * TILES, D]), ALU.mult)

                def twice_derivative(s, c, made, done):
                    stt(c[:, k], s[:, k], 1.0, c[:, k], ALU.subtract, ALU.mult).then_inc(made, 1)
                    dve.wait_ge(made, i + 1)
                    return stt(c[:, k], s[:, k], 1.0, c[:, k], ALU.add, ALU.subtract).then_inc(done, 1)

                if real(i - 2):
                    dve.wait_ge(dz0t_done, i - 1)
                    if since(i, 4):
                        dve.wait_ge(gw_done, i - 3)
                    turned_out_of(A_DZ0T, i - 2, (k, 0)).then_inc(dz0t_out, 1)
                if real(i):
                    dve.wait_ge(t0_done, i + 1)
                    twice_derivative(s0, c0, m0_done, c0_done)
                    dve.wait_ge(t1_done, i + 1)
                    twice_derivative(s1, c1, m1_done, c1_done)
                if real(i - 1):
                    dve.wait_ge(back_done, i)
                    dve.wait_ge(dz1_done, i)
                    stt(dd[:, other], A_BACK[:, :], 0.5, dd[:, other], ALU.mult, ALU.add).then_inc(dy_done, 1)
                if real(i):
                    dve.wait_ge(d_done, i + 1)
                    dve.wait_ge(ss_done, i + 1)
                    tt(dd[:, k], A_D[:, :], dd[:, k], ALU.add).then_inc(dd_done, 1)
                    dve.wait_ge(dd_done, i + 1)
                    dve.wait_ge(c1_done, i + 1)
                    tt(c1[:, k], dd[:, k], c1[:, k], ALU.mult).then_inc(dz1_done, 1)
                if real(i - 1):
                    dve.wait_ge(dz1t_done, i)
                    if since(i, 3):
                        dve.wait_ge(gw_done, i - 2)
                    turned_out_of(A_DZ1T, i - 1, (other, 1)).then_inc(dz1t_out, 1)

            learn(0, 0)
            dve.wait_ge(alr_t, 1)
            ts(alr[:, :, 0], alr[:, :, 0], MAX_ALR / D / 2, MAX_ALR / D / 2, ALU.mult, ALU.add).then_inc(alr_done, 1)
            dve.wait_ge(alr_done, 1)
            steps(dve, 2, 2, learn, done=1)

            old = W[:, AT["w0_dd"][0]:AT["b1_dd"][1]]
            dve.wait_ge(gw_done, B)
            nc.vector.tensor_copy(grad_s[:, :], A_G[:, 0:XW]).then_inc(learn_dve, 1)
            dve.wait_ge(learn_pe, 1)
            nc.vector.tensor_copy(gradt_s[:, :], A_Z0[:, 0:128]).then_inc(learn_dve, 1)
            dve.wait_ge(learn_pe, 2)
            g = A_Z1[:, 0:130]
            ts(adam[:, 0], g, -1.0, None, ALU.mult).then_inc(learn_dve, 1)
            dve.wait_ge(learn_dve, 3)
            tt(adam[:, 1], g, adam[:, 0], ALU.max).then_inc(learn_dve, 1)
            dve.wait_ge(learn_dve, 4)
            ts(adam[:, 1], adam[:, 1], ADAM_EPS, None, ALU.add).then_inc(learn_dve, 1)
            dve.wait_ge(learn_dve, 5)
            nc.vector.reciprocal(adam[:, 2], adam[:, 1]).then_inc(learn_dve, 1)
            dve.wait_ge(learn_dve, 6)
            stt(adam[:, 0], adam[:, 0], LR, adam[:, 2], ALU.mult, ALU.mult).then_inc(learn_dve, 1)
            dve.wait_ge(learn_dve, 7)
            stt(params[:, :], old, 1.0 - LR * WD, adam[:, 0], ALU.mult, ALU.add).then_inc(learn_dve, 1)
            dve.wait_ge(learn_dve, 8)
            for h in range(2):
                part, at_h = slice(64 * h, 64 * h + 64), slice(64 * h, 64 * h + 64)
                nc.vector.tensor_copy(n1_bd[part, at_h], params[part, 64:128]).then_inc(learn_dve, 1)
            dve.wait_ge(learn_pe, 3)
            for h in range(2):
                part, at_h = slice(64 * h, 64 * h + 64), slice(64 * h, 64 * h + 64)
                nc.vector.tensor_copy(r_w[part, at_h], A_D[part, 0:D]).then_inc(learn_dve, 1)

            def retrieve(i, k):
                par = k % 2
                if real(i):
                    dve.wait_ge(rq_done, i + 1)
                    dve.wait_ge(p0_done, i + 1)
                    if since(i, 2):
                        dve.wait_ge(rz1_done, i - 1)
                        dve.wait_ge(h2_done, i - 1)
                    tt(y1[:, par], R_Q[par][:, :], p0[:, par], ALU.add).then_inc(y1_done, 1)
                if real(i - 1):
                    dve.wait_ge(hs_done, i)
                    dve.wait_ge(y1_done, i)
                    if since(i, 5):
                        dve.wait_ge(h2t_done, i - 4 + par)
                    tt(h2_of((k - 1) % 4), by(hs[:, 1 - par], V), by(y1[:, 1 - par], V), ALU.add).then_inc(h2_done, 1)
                if par == 1 and since(i, 3):
                    for q in range(2):
                        dve.wait_ge(h2t_done, i - 2 + q)
                        nc.vector.tensor_copy(cols(resid, i - 3 + q), R_T[q][:, :]).then_inc(h2t_out, 1)

            steps(dve, 2, 4, retrieve)

            dve.wait_ge(h2t_out, B)

            def route_experts(i, k):
                par = k % 2
                if par == 0 and real(i):
                    n = i // 2
                    total, sq_total, root, rate = (stats[:, m, 0] for m in range(4))
                    tokens = cols(resid, n, NP * D).rearrange("p (n d) -> p n d", d=D)
                    if since(i, 2):
                        dve.wait_ge(centred2, n)
                    reduce(total, tokens, AX.X, ALU.add).then_inc(summed2, 1)
                    dve.wait_ge(summed2, n + 1)
                    if since(i, 2):
                        dve.wait_ge(normed2, n)
                    stt(cen2, each(total), -1 / D, tokens, ALU.mult, ALU.add).then_inc(centred2, 1)
                if since(i, 4):
                    s = (k - par) // 2
                    if par == 0 and since(i, 8):
                        dve.wait_ge(out_dma[s], 4 * i - 16 - 8 * s)
                    dve.wait_ge(wo_done, i - 3)
                    if par == 0:
                        dve.wait_ge(biased, (i - 2) // 2)
                    tt(outs[:, s, par * COLS:(par + 1) * COLS], E_O[par][:, :], cols(resid, i - 4), ALU.add
                       ).then_inc(out_added, 1)
                if par == 0 and real(i):
                    dve.wait_ge(squared2, n + 1)
                    reduce(sq_total, sq2, AX.X, ALU.add).then_inc(sq_summed2, 1)
                    dve.wait_ge(rooted2, n + 1)
                    nc.vector.reciprocal(rate, root).then_inc(rate2_done, 1)
                    dve.wait_ge(rate2_done, n + 1)
                    dve.wait_ge(centred2, n + 1)
                    if since(i, 2):
                        dve.wait_ge(turned2, i)
                    tt(xh2, cen2, each(rate), ALU.mult).then_inc(normed2, 1)

            steps(dve, 4, 4, route_experts, 2 * FRONT)

        @block.gpsimd
        def _(pool):
            tt, ts = nc.gpsimd.tensor_tensor, nc.gpsimd.tensor_scalar

            def across(row, n):
                return row.rearrange("p (a d) -> p a d", a=1).to_broadcast([128, n, D])

            pool.wait_ge(tokw_in, 16)
            tt(tails, freq_w[:, :, 0], coef[:, :, HALF].to_broadcast([128, 2 * ROUNDS, D]), ALU.mult).then_inc(tail_done, 1)
            n = ROUNDS
            while n:
                pool.wait_ge(tail_done, 1 + (ROUNDS // n).bit_length() - 1)
                tt(tails[:, 0:n], tails[:, 0:n], tails[:, n:2 * n], ALU.add).then_inc(tail_done, 1)
                n //= 2
            for buffer in (z_w, r_w, n1_bd):
                last = nc.gpsimd.memset(buffer[:], 0.0)
            last.then_inc(zeroed, 1)
            nc.gpsimd.memset(eps[:], LN_EPS)
            nc.gpsimd.memset(odd_s[:, :, COLS - V:], 0.0)
            pool.wait_ge(w_in, 16)
            ts(half_b[:, 0:2], W[:, AT["b0_dd"][0]:AT["b1_dd"][1]], 0.5, 0.0, ALU.mult, ALU.add)
            ts(half_b[:, 2:3], w["blr"], 0.5, 0.0, ALU.mult, ALU.add)
            tt(d_w[:, :], w["wk_bd"], w["wv_bd"], ALU.subtract)
            for name in ("ws0", "ws1"):
                last = tt(w[name][:, 0:HID], w[name][:, 0:HID], w["ident"], ALU.add)
            last.then_inc(setup_pool, 1)
            nc.gpsimd.memset(rows3[:, :, 2 * D:], 1.0).then_inc(setup_pool, 1)

            def tokenize(i, k):
                other = 1 - k
                if real(i):
                    pool.wait_ge(added, i + 1)
                    nc.gpsimd.tensor_copy(cols(hT, i), h_new[:, k]).then_inc(kept, 1)
                if real(i - 1):
                    pool.wait_ge(normed, i)
                    if since(i, 3):
                        pool.wait_ge(logit_done, i - 2)
                    tt(by(xlr[:, other], D), by(xh[:, other], D), across(w["wlr_row"], NJ), ALU.mult).then_inc(xlr_done, 1)

            steps(pool, 1, 2, tokenize)

            def learn(i, k):
                other = 1 - k
                if real(i):
                    pool.wait_ge(s1_done, i + 1)
                    if since(i, 2):
                        pool.wait_ge(dz0_done, i - 1)
                    tt(dd[:, k], s0[:, k], s1[:, k], ALU.add).then_inc(ss_done, 1)
                if real(i - 1):
                    pool.wait_ge(dy_done, i)
                    pool.wait_ge(c0_done, i)
                    if since(i, 3):
                        pool.wait_ge(dz0t_done, i - 2)
                    tt(dz0[:, other], dd[:, other], c0[:, other], ALU.mult).then_inc(dz0_done, 1)

            steps(pool, 1, 2, learn)

            def retrieve(i, k):
                par = k % 2
                if real(i - 1):
                    pool.wait_ge(p1_done, i)
                    if since(i, 3):
                        pool.wait_ge(h2_done, i - 2)
                    tt(hs[:, 1 - par], cols(hT, i - 1), p1[:, 1 - par], ALU.add).then_inc(hs_done, 1)

            steps(pool, 1, 2, retrieve)

            pool.wait_ge(wr_in, 16)
            pool.wait_ge(route_step, 6)

            def route_experts(i, k):
                if real(i):
                    if since(i, 2):
                        pool.wait_ge(l2_done, 2 * i - 2)
                        pool.wait_ge(hF_ready, 2 * i - 2)
                    for g in range(GROUPS):
                        e = pool.value_load(route_ix[0:1, bass.ds(i * GROUPS + g, 1)], min_val=0, max_val=EXPERTS)
                        for l, name in enumerate(("ws0", "ws1")):
                            last = tt(wuse[:, l, k * GROUPS + g], wr[:, l, bass.ds(e, 1)].rearrange("p o n -> p (o n)"),
                                      w[name], ALU.add)
                    last.then_inc(wuse_ready, 1)

                if k % 2 == 1:
                    pool.wait_ge(centred2, (i + 1) // 2)
                    pair = cols(resid, (i - 1) // 2, NP * D).rearrange("p (n d) -> p n d", d=D)
                    tt(pair, pair, across(w["bo"], NP), ALU.add).then_inc(biased, 1)

            steps(pool, 0, 2, route_experts)


def packed(inputs):
    def f(name):
        return np.asarray(inputs[name])

    eye, zero = np.eye(64, dtype=np.float32), np.zeros((64, 64), np.float32)

    def bd(a):
        return np.block([[a, zero], [zero, a]])

    def down(a):
        return np.concatenate([a, a], 0)

    wk, wq, wv, w1 = f("L0_attn_Wk"), f("L0_attn_Wq"), f("L0_attn_Wv"), f("L0_attn_Ws")[1]
    wlr = f("L0_attn_Wlr")
    ws, bs = f("L0_ffn_Ws"), f("L0_ffn_bs")
    wi, none = f("L0_ffn_Wi"), np.zeros((D, HID), np.float32)
    parts = {
        "wk_bd": bd(wk), "wv_bd": bd(wv), "wq_bd": bd(wq), "w1_bd": bd(w1), "w1t_bd": bd(w1.T),
        "wkt_dd": np.block([[wk.T, wk.T], [zero, zero]]), "wqt_dd": np.block([[wq.T, wq.T], [zero, zero]]),
        "grad0": np.block([[wk, wk], [zero, zero]]), "grad1": np.block([[wk, wk], [eye, eye]]),
        "w0_dd": down(f("L0_attn_Ws")[0]), "w1_dd": down(w1),
        "b0_dd": down(f("L0_attn_bs")[0][:, None]), "b1_dd": down(f("L0_attn_bs")[1][:, None]),
        "wlr_row": np.tile(wlr.T, (128, 1)),
        "blr": np.tile(f("L0_attn_blr")[None, :], (128, 1)),
        "wi0": np.concatenate([wi.T, none], 0), "wi1": np.concatenate([none, wi.T], 0),
        "bi": f("L0_ffn_bi")[:, None],
        "ws0": np.concatenate([ws[0, 0].T, bs[0, 0][:, None]], 1),
        "ws1": np.concatenate([ws[1, 0].T, bs[1, 0][:, None]], 1),
        "wot": f("L0_ffn_Wo").T, "bo": np.tile(f("L0_ffn_bo")[None, :], (128, 1)),
        "ident": np.eye(128, dtype=np.float32),
        "spread0": np.block([[eye, eye], [zero, zero]]), "spread1": np.block([[zero, zero], [eye, eye]]),
    }
    return np.ascontiguousarray(np.concatenate([parts[n] for n, _ in PACK], 1))


def kernel(**inputs):
    import concourse.bacc as bacc
    from concourse.bass_utils import run_bass_kernel_spmd

    tokw = np.asarray(inputs["L0_tok_W"]).reshape(D, 2, 9, C)
    order = [pf for pair in zip(EVEN, ODD) for pf in pair]
    tokw = np.concatenate([tokw[:, part, f].T for part, f in order], 1)
    wr, br = np.asarray(inputs["L0_ffn_Wr"]), np.asarray(inputs["L0_ffn_br"])
    experts = np.zeros((HID, LAYERS, EXPERTS + 1, WE), wr.dtype)
    experts[:, :, :EXPERTS, :HID] = wr.transpose(3, 0, 1, 2)
    experts[:, :, :EXPERTS, HID] = br.transpose(2, 0, 1)
    arrays = {
        "x": np.ascontiguousarray(inputs["x"]),
        "tokw": np.concatenate([np.concatenate([tokw, tokw], 0), fold_table()], 1),
        "pack": packed(inputs),
        "experts": experts.reshape(HID, -1),
        "route": np.ascontiguousarray(inputs["L0_ffn_route_id"]).reshape(1, -1),
    }
    nc = bacc.Bacc("TRN2", target_bir_lowering=False, num_devices=1)
    args = [nc.dram_tensor(n, a.shape, mybir.dt.from_np(a.dtype), kind="ExternalInput").ap()
            for n, a in arrays.items()]
    out = nc.dram_tensor("out", (B, V * NP, D), F32, kind="ExternalOutput").ap()
    tower(nc, *args, out)
    r = run_bass_kernel_spmd(nc, [arrays], core_ids=[0])
    return r.results[0]["out"]
```

```python
from contextlib import ExitStack

import numpy as np

import concourse.bass as bass
from concourse import mybir

F32 = mybir.dt.float32
F32R = mybir.dt.float32r
I32 = mybir.dt.int32
ALU = mybir.AluOpType
ACT = mybir.ActivationFunctionType
AX = mybir.AxisListType

B, C, T, V = 16, 64, 128, 64
D = 64
PATCH, STRIDE = 16, 8
NP = T // STRIDE
NJ = NP // 2
COLS = NJ * V
TILES = COLS // 128
HALF = STRIDE // 2
HID, EXPERTS, LAYERS = 128, 16, 2
GROUPS = 4
GV = V // GROUPS
GC = NP * GV
XW = 2 * D + 1
WE = HID + 1
LR, WD, MAX_ALR, ADAM_EPS, LN_EPS = 1e-3, 0.01, 0.1, 1e-8, 1e-5

PACK = [
    ("wk_bd", 128), ("wv_bd", 128), ("wq_bd", 128), ("w1_bd", 128), ("w1t_bd", 128),
    ("wkt_dd", 128), ("wqt_dd", 128), ("grad0", 128), ("grad1", 128),
    ("w0_dd", 64), ("w1_dd", 64), ("b0_dd", 1), ("b1_dd", 1),
    ("wlr_row", 64), ("blr", 1), ("wi0", 128), ("wi1", 128), ("bi", 1),
    ("ws0", WE), ("ws1", WE), ("wot", 64), ("bo", 64),
    ("ident", 128), ("spread0", 128), ("spread1", 128),
]
AT = {}
_at = 0
for _name, _w in PACK:
    AT[_name] = (_at, _at + _w)
    _at += _w
PACKED = _at

COEFS = [(0, f) for f in range(PATCH // 2 + 1)] + [(1, f) for f in range(1, PATCH // 2)]
FOLD_OUT = 128 // len(COEFS)
FOLDS = D // FOLD_OUT
FOLD_W = (2 * STRIDE + 1) * FOLD_OUT


def dft(part, f, k):
    a = 2 * np.pi * f * k / PATCH
    return (np.cos(a) if part == 0 else -np.sin(a)) / np.sqrt(PATCH)


def fold_table():
    t = np.zeros((len(COEFS), FOLD_OUT, 2 * STRIDE + 1, FOLD_OUT))
    for n, (part, f) in enumerate(COEFS):
        of = [dft(part, f, k) for k in range(PATCH)]
        for o in range(FOLD_OUT):
            t[n, o, :, o] = of[STRIDE:] + of[:STRIDE] + [sum(of[STRIDE - 1:])]
    t[abs(t) < 1e-12] = 0.0
    return t.astype(np.float32).reshape(128, -1)


FRONT = 4


def steps(eng, lag, unroll, step, front=FRONT, done=0, end=B):
    for i in range(done, front):
        step(i, i % unroll)
    with eng.Fori(0, (end - front) // unroll) as n:
        for k in range(unroll):
            step(n * unroll + front + k, (front + k) % unroll)
    for i in range(end, B + lag):
        step(i, i % unroll)


def real(c, n=B):
    return not isinstance(c, int) or 0 <= c < n


def since(c, first):
    return not isinstance(c, int) or c >= first


def tower(nc, x, tokw, pack, experts, route, out):
    ctx = ExitStack()
    with ctx:
        def sb(name, shape, dt=F32):
            return ctx.enter_context(nc.sbuf_tensor(name, shape, dt))

        def sem(name):
            return ctx.enter_context(nc.semaphore(name))

        hT = sb("hT", [128, B * COLS])
        x_hi = sb("x_hi", [128, B * COLS], F32R)
        x_lo = sb("x_lo", [128, B * COLS], F32R)
        rows = sb("rows", [128, B * COLS])
        W = sb("W", [128, PACKED])
        w = {n: W[:, a:b] for n, (a, b) in AT.items()}
        tokw_sb = hT[:, 0:FOLDS * 128 + FOLD_W]
        table_at = FOLDS * 128
        patch_w = sb("patch_w", [128, HALF, 3, D])
        patch_end = sb("patch_end", [128, 2 * D])
        key_value = hT[:, tokw_sb.shape[1]:tokw_sb.shape[1] + 128]
        z_w = sb("z_w", [128, 2, 2, 128], F32R)
        d_w, q_w, r_w = (sb(n, [128, 2, 128], F32R) for n in ("d_w", "q_w", "r_w"))
        wi_w = sb("wi_w", [128, 2, 2, 128], F32R)
        n1_bd = sb("n1_bd", [128, 128])
        logit = sb("logit", [128, B * TILES * 2])
        alr = sb("alr", [128, B * TILES * 2, 1])
        half_b = sb("half_b", [128, 3])
        eps = sb("eps", [128, 1])
        stats = sb("stats", [128, 4, 2, NP])
        grad_s = sb("grad_s", [128, XW])
        gradt_s = sb("gradt_s", [128, 128])
        adam = sb("adam", [128, 3, 130])
        params = sb("params", [128, 130])
        route_sb = sb("route_sb", [1, B * GROUPS], I32)
        route_f = sb("route_f", [1, 4, B * GROUPS])
        route_ix = sb("route_ix", [1, B * GROUPS], I32)

        arena = sb("arena", [128, 13 * 1024])
        at = [0]

        def scratch(*shape):
            n = int(np.prod(shape))
            a = arena[:, at[0]:at[0] + n]
            at[0] += n
            if len(shape) == 2:
                return a.rearrange("p (a b) -> p a b", b=shape[1])
            if len(shape) == 3:
                return a.rearrange("p (a b c) -> p a b c", b=shape[1], c=shape[2])
            return a

        xb = scratch(2, 2 * NJ, HALF * V)
        odd_s = scratch(2, COLS)
        h_new, cen, xh = (scratch(2, COLS) for _ in range(3))
        sq, xlr = scratch(COLS), scratch(COLS)
        at[0] = 0
        s0, c0, s1, c1, dd, dz0 = (scratch(2, COLS) for _ in range(6))
        dzt = scratch(2, 2 * TILES, 2 * D)
        factors = scratch(2, 2 * TILES, XW)
        at[0] = 0
        p0, p1, hs, y1 = (scratch(2, COLS) for _ in range(4))
        h2 = scratch(2, NJ, 2 * V)
        at[0] = 0
        outs = scratch(2, NP * D)
        hid0, hid1 = (scratch(NP * V) for _ in range(2))
        hidF = scratch(2, NP, 2 * V)
        cen2, sq2, xh2 = (scratch(NP, D) for _ in range(3))
        resid = rows
        x2_hi, x2_lo = (a[:, 0:4 * COLS].rearrange("p (s j n) -> p s j n", s=2, j=NJ) for a in (x_hi, x_lo))
        e1 = LAYERS * (EXPERTS + 1) * WE
        wr = hT[:, 0:e1].rearrange("p (l e n) -> p l e n", l=LAYERS, n=WE)
        e2 = e1 + LAYERS * 2 * GROUPS * WE
        assert e2 <= B * COLS
        wuse = hT[:, e1:e2].rearrange("p (l s n) -> p l s n", l=LAYERS, n=WE)

        bank = [ctx.enter_context(nc.psum_tensor(f"bank{n}", [128, COLS], F32)) for n in range(8)]

        def by(ap, n):
            return ap.rearrange("p (a n) -> p a n", n=n)

        x_in = [sem("x_in0"), sem("x_in1")]
        w_in, tokw_in, wr_in, route_in = sem("w_in"), sem("tokw_in"), sem("wr_in"), sem("route_in")
        fold_pe = sem("fold_pe")
        zeroed, folded, setup_pe, setup_act, setup_pool = (
            sem(n) for n in ("zeroed", "folded", "setup_pe", "setup_act", "setup_pool"))
        odd_done, even_done, odd_out, added, turned, summed, centred, squared = (
            sem(n) for n in ("odd_done", "even_done", "odd_out", "added", "turned", "summed",
                             "centred", "squared"))
        sq_summed, rooted, rate_done, normed, in_rows, xlr_done, logit_done, back_turned, stored = (
            sem(n) for n in ("sq_summed", "rooted", "rate_done", "normed", "in_rows", "xlr_done",
                             "logit_done", "back_turned", "stored"))
        hi_stored, x_out, ones_set = sem("hi_stored"), sem("x_out"), sem("ones_set")
        kept, split_done = sem("kept"), sem("split_done")
        pool_split = sem("pool_split")
        alr_t, alr_done = sem("alr_t"), sem("alr_done")
        z0_done, d_done, z1_done, s0_done, t0_done, s1_done, t1_done = (
            sem(n) for n in ("z0_done", "d_done", "z1_done", "s0_done", "t0_done", "s1_done", "t1_done"))
        m0_done, c0_done, m1_done, c1_done, ss_done, dd_done, dz1_done = (
            sem(n) for n in ("m0_done", "c0_done", "m1_done", "c1_done", "ss_done", "dd_done", "dz1_done"))
        back_done, dy_done, dz0_done, s0t_done, s0t_out, dz1t_done, dz1t_out, dz0t_done, dz0t_out = (
            sem(n) for n in ("back_done", "dy_done", "dz0_done", "s0t_done", "s0t_out", "dz1t_done",
                             "dz1t_out", "dz0t_done", "dz0t_out"))
        gw_done, learn_pe, learn_dve = sem("gw_done"), sem("learn_pe"), sem("learn_dve")
        rz0_done, rq_done, rz1_done, p0_done, p1_done, hs_done, y1_done, h2_done = (
            sem(n) for n in ("rz0_done", "rq_done", "rz1_done", "p0_done", "p1_done", "hs_done",
                             "y1_done", "h2_done"))
        h2t_done, h2t_out = sem("h2t_done"), sem("h2t_out")
        summed2, centred2, squared2, sq_summed2, rooted2, rate2_done, normed2, turned2, biased = (
            sem(n) for n in ("summed2", "centred2", "squared2", "sq_summed2", "rooted2", "rate2_done",
                             "normed2", "turned2", "biased"))
        x2_hi_done, x2_done = sem("x2_hi_done"), sem("x2_done")
        in_done, l1_done, l2_done, h0_ready, h1_ready, hF_ready = (
            sem(n) for n in ("in_done", "l1_done", "l2_done", "h0_ready", "h1_ready", "hF_ready"))
        wo_done, out_added, wuse_ready, route_step = (
            sem(n) for n in ("wo_done", "out_added", "wuse_ready", "route_step"))
        out_dma = [sem("out_dma0"), sem("out_dma1")]

        P_ODD, P_EVEN, P_H, P_X, P_W = bank[0:2], bank[2], bank[3], bank[5], bank[7]
        F_W = bank[3], bank[4], bank[6]
        A_Z0, A_Z1, A_D, A_BACK, A_S0T, A_DZ1T, A_DZ0T, A_G = bank
        R_Z0, R_Q, R_Z1, R_T = bank[0:2], bank[2:4], bank[4], bank[5:7]
        E_O, E_X, E_H = bank[0:2], bank[2:4], bank[4:8]

        xs = x.rearrange("b c (m h t) v -> b h c m (t v)", h=2, t=HALF)
        out_rows = out.rearrange("b (v n) d -> (b v) (n d)", n=NP)

        def cols(tensor, c, n=COLS):
            return tensor[:, bass.ds(c * n, n)]

        def h2_of(k):
            return h2[:, k // 2].rearrange("p j (b v) -> p b j v", b=2)[:, k % 2]

        def half_of(a, k, q):
            return a[:, k // 2, q * NJ // 2:(q + 1) * NJ // 2].rearrange("p a b -> p (a b)")

        block = ctx.enter_context(nc.Block())

        @block.sync
        def _(sp):
            def load_x(i, k):
                if since(i, 2):
                    sp.wait_ge(even_done, i - 1)
                for h in range(2):
                    sp.dma_start(xb[64 * h:64 * h + 64, k], xs[bass.ds(i, 1), h].rearrange("o c m n -> c (o m) n")
                                 ).then_inc(x_in[k], 16)

            sp.dma_start(tokw_sb, tokw).then_inc(tokw_in, 16)
            load_x(0, 0)
            sp.dma_start(W[:, :], pack).then_inc(w_in, 16)
            load_x(1, 1)
            sp.dma_start(route_sb[:], route).then_inc(route_in, 16)
            with sp.Fori(1, B // 2) as n:
                for k in range(2):
                    load_x(2 * n + k, k)
            sp.wait_ge(hs_done, -(-e1 // COLS))
            sp.dma_start(hT[:, 0:e1], experts).then_inc(wr_in, 16)

            def store(p, s, row):
                for q in range(2):
                    sp.wait_ge(out_added, 2 * p + q + 1)
                    half = slice(q * COLS, (q + 1) * COLS)
                    sp.dma_start(out_rows[bass.ds(row, 128), half], outs[:, s, half]).then_inc(out_dma[s], 16)

            with sp.Fori(0, B // 4) as n:
                for s in range(2):
                    store(2 * n + s, s, n * 256 + s * 128)
            for s in range(2):
                sp.wait_ge(out_dma[s], 2 * 16 * (B // 4))

        @block.tensor
        def _(pe):
            mm, tr = nc.tensor.matmul, nc.tensor.transpose

            def product(out, weight, i, stop=True):
                mm(out, weight[1], cols(x_hi, i), start=True, stop=False)
                mm(out, weight[0], cols(x_lo, i), start=False, stop=False)
                return mm(out, weight[0], cols(x_hi, i), start=False, stop=stop)

            pe.wait_ge(tokw_in, 16)
            for n in range(FOLDS):
                last = mm(F_W[n // 3][:, n % 3 * FOLD_W:(n % 3 + 1) * FOLD_W], tokw_sb[:, 128 * n:128 * n + 128],
                          tokw_sb[:, table_at:], start=True, stop=True)
            last.then_inc(fold_pe, 1)

            pe.wait_ge(folded, 2)

            def tokenize(i, k):
                k = k % 2
                if real(i):
                    pe.wait_ge(x_in[k], 16 * (i - k) + 32)
                    if since(i, 2):
                        pe.wait_ge(added, i - 1)
                    xm = xb[:, k].rearrange("p (j o) (t v) -> p j o t v", o=2, t=HALF)
                    for t in (0, HALF - 1, *range(1, HALF - 1)):
                        lhs = patch_w[:, t, 0:2].rearrange("p a b -> p (a b)")
                        if t < HALF - 1:
                            last = mm(P_ODD[k][:, :], lhs, xm[:, :, 1, t], start=(t == 0), stop=(t == HALF - 2))
                        else:
                            mm(P_ODD[k][:, 0:COLS - V], lhs, xm[:, 0:NJ - 1, 1, t], start=False, stop=False,
                               skip_group_check=True)
                            mm(P_ODD[k][:, COLS - V:], patch_end[:, :], xm[:, NJ - 1, 1, t], start=False,
                               stop=False, skip_group_check=True)
                    last.then_inc(odd_done, 1)
                if real(i - 1):
                    pe.wait_ge(added, i)
                    if since(i, 2):
                        pe.wait_ge(centred, i - 1)
                    for t in range(TILES):
                        last = tr(P_H[:, 128 * t:128 * t + 128], h_new[:, 1 - k, 128 * t:128 * t + 128], w["ident"])
                    last.then_inc(turned, 1)
                if real(i - 2):
                    pe.wait_ge(normed, i - 1)
                    if since(i, 3):
                        pe.wait_ge(stored, i - 2)
                    for t in range(TILES):
                        last = tr(P_X[:, 128 * t:128 * t + 128], xh[:, k, 128 * t:128 * t + 128], w["ident"])
                    last.then_inc(back_turned, 1)
                if real(i):
                    if since(i, 1):
                        pe.wait_ge(odd_out, i)
                    else:
                        pe.wait_ge(folded, 3)
                    for t in range(HALF):
                        last = mm(P_EVEN[:, :], patch_w[:, t, 1:3].rearrange("p a b -> p (a b)"),
                                  xm[:, :, 0, t], start=(t == 0), stop=(t == HALF - 1))
                    last.then_inc(even_done, 1)

            tokenize(0, 0)
            pe.wait_ge(w_in, 16)
            mm(P_W[:, 0:64], w["wkt_dd"][0:64], w["w0_dd"][0:64], start=True, stop=True)
            mm(P_W[:, 64:128], w["wkt_dd"][0:64], w["w1_dd"][0:64], start=True, stop=True).then_inc(setup_pe, 1)
            steps(pe, 1, 2, tokenize, done=1)

            pe.wait_ge(added, B)
            pe.wait_ge(setup_pool, 1)
            pe.wait_ge(split_done, 1)

            def learn(i, k):
                other = 1 - k
                if real(i):
                    pe.wait_ge(stored, i + 1)
                    if since(i, 1):
                        pe.wait_ge(t0_done, i)
                    product(A_Z0[:, :], [z_w[:, part, 0] for part in range(2)], i).then_inc(z0_done, 1)
                if real(i - 1):
                    if since(i, 2):
                        pe.wait_ge(s0t_out, i - 1)
                    for t in range(TILES):
                        tile = slice(128 * t, 128 * t + 128)
                        last = tr(A_S0T[:, tile], s0[:, other, tile], w["ident"])
                    last.then_inc(s0t_done, 1)
                if real(i):
                    if since(i, 1):
                        pe.wait_ge(dd_done, i)
                    product(A_D[:, :], [d_w[:, part] for part in range(2)], i).then_inc(d_done, 1)
                if real(i - 2):
                    pe.wait_ge(dz0_done, i - 1)
                    if since(i, 3):
                        pe.wait_ge(dz0t_out, i - 2)
                    for t in range(TILES):
                        tile = slice(128 * t, 128 * t + 128)
                        last = tr(A_DZ0T[:, tile], dz0[:, k, tile], w["ident"])
                    last.then_inc(dz0t_done, 1)
                if real(i):
                    if since(i, 1):
                        pe.wait_ge(t1_done, i)
                    product(A_Z1[:, :], [z_w[:, part, 1] for part in range(2)], i, stop=False)
                    pe.wait_ge(s0_done, i + 1)
                    mm(A_Z1[:, :], w["w1_bd"], s0[:, k], start=False, stop=True).then_inc(z1_done, 1)

                def gradient():
                    if real(i - 2):
                        pe.wait_ge(s0t_out, i - 1)
                        pe.wait_ge(x_out, i - 1)
                        pe.wait_ge(dz0t_out, i - 1)
                        pe.wait_ge(dz1t_out, i - 1)
                        for t in range(2 * TILES):
                            first = isinstance(i, int) and i == 2 and t == 0
                            final = isinstance(i, int) and i == B + 1 and t == 2 * TILES - 1
                            last = mm(A_G[:, 0:XW], dzt[:, k, t], factors[:, k, t],
                                      start=first, stop=final, skip_group_check=True)
                        last.then_inc(gw_done, 1)

                def backward():
                    if real(i - 1):
                        pe.wait_ge(dz1_done, i)
                        if since(i, 2):
                            pe.wait_ge(dy_done, i - 1)
                        else:
                            pe.wait_ge(stored, B)
                        mm(A_BACK[:, :], w["w1t_bd"], c1[:, other], start=True, stop=True).then_inc(back_done, 1)
                        if since(i, 2):
                            pe.wait_ge(dz1t_out, i - 1)
                        for t in range(TILES):
                            tile = slice(128 * t, 128 * t + 128)
                            last = tr(A_DZ1T[:, tile], c1[:, other, tile], w["ident"])
                        last.then_inc(dz1t_done, 1)

                for part in ((backward, gradient) if isinstance(i, int) and i == B else (gradient, backward)):
                    part()

            for i in range(2):
                learn(i, i)
                if i == 0:
                    tokenize(B + 1, 1)
                    pe.wait_ge(setup_act, 1)
            steps(pe, 2, 2, learn, done=2)

            def queries(i, par):
                product(R_Q[par][:, :], [q_w[:, part] for part in range(2)], i).then_inc(rq_done, 1)

            pe.wait_ge(learn_dve, 1)
            tr(A_Z0[:, 0:128], grad_s[:, 0:128], w["ident"]).then_inc(learn_pe, 1)
            mm(A_Z1[:, 128:129], w["spread0"], grad_s[:, 128:129], start=True, stop=True)
            mm(A_Z1[:, 129:130], w["spread1"], grad_s[:, 128:129], start=True, stop=True)
            pe.wait_ge(learn_dve, 2)
            mm(A_Z1[:, 0:64], w["grad0"], gradt_s[:, 0:64], start=True, stop=True)
            mm(A_Z1[:, 64:128], w["grad1"], gradt_s[:, 64:128], start=True, stop=True).then_inc(learn_pe, 1)
            for i in range(2):
                queries(i, i)
            pe.wait_ge(learn_dve, 8)
            mm(A_S0T[:, 0:D], w["wqt_dd"][0:64], params[0:64, 0:D], start=True, stop=True).then_inc(learn_pe, 1)
            pe.wait_ge(learn_dve, 12)

            def retrieve(i, k):
                other = 1 - k % 2
                if real(i):
                    if since(i, 2):
                        pe.wait_ge(p0_done, i - 1)
                    product(R_Z0[k % 2][:, :], [r_w[:, part] for part in range(2)], i).then_inc(rz0_done, 1)
                    if since(i, 2):
                        pe.wait_ge(y1_done, i - 1)
                        queries(i, k % 2)
                if isinstance(i, int) and i == 1:
                    pe.wait_ge(learn_dve, 14)
                if real(i - 1):
                    pe.wait_ge(y1_done, i)
                    if since(i, 2):
                        pe.wait_ge(p1_done, i - 1)
                    mm(R_Z1[:, :], n1_bd[:, :], y1[:, other], start=True, stop=True).then_inc(rz1_done, 1)
                if k % 2 == 0 and since(i, 4):
                    pe.wait_ge(h2_done, i - 2)
                    if since(i, 6):
                        pe.wait_ge(h2t_out, i - 4)
                    pair = k // 2
                    for q in range(2):
                        for j in range(NJ // 2):
                            last = tr(R_T[q][:, 128 * j:128 * j + 128], h2[:, pair, q * NJ // 2 + j], w["ident"])
                        last.then_inc(h2t_done, 1)

            steps(pe, 3, 4, retrieve, 2 * FRONT)

            pe.wait_ge(h2t_out, B)

            def turn(i):
                pe.wait_ge(normed2, (i + 1) // 2)
                if since(i, 3):
                    pe.wait_ge(x2_done, i - 1)
                for j in range(NJ):
                    tile = xh2[:, 2 * j:2 * j + 2].rearrange("p a b -> p (a b)")
                    last = tr(E_X[j // 4][:, j % 4 * 128:(j % 4 + 1) * 128], tile, w["ident"])
                    if j % 4 == 3:
                        last.then_inc(turned2, 1)

            def route_experts(i, k):
                par = k % 2
                first, second = 2 * par, 2 * (1 - par)

                def output(part):
                    if not since(i, 4):
                        return
                    if par == 0 and part == 0:
                        pe.wait_ge(hF_ready, 2 * i - 4)
                    if part == 0 and since(i, 6):
                        pe.wait_ge(out_added, i - 5)
                    for n in range(part * NJ // 2, (part + 1) * NJ // 2):
                        last = mm(E_O[par][:, n * D:(n + 1) * D], hidF[:, (k - par) // 2, NJ * par + n], w["wot"],
                                  start=True, stop=True)
                    if part:
                        last.then_inc(wo_done, 1)

                if real(i - 2):
                    pe.wait_ge(x2_done, i - par)
                    if since(i, 3):
                        pe.wait_ge(h1_ready, 2 * i - 4)
                    hi, lo = (a[:, (k + 2) % 4 // 2].rearrange("p j (b g v) -> p b g j v", b=2, v=GV)[:, par]
                              for a in (x2_hi, x2_lo))
                    for b in range(2):
                        hv = E_H[first + b][:, :].rearrange("p (g r j v) -> p r g j v", g=2, r=2, v=GV)
                        for r in range(2):
                            mm(hv[:, r], wi_w[:, 1, r], hi[:, 2 * b:2 * b + 2], start=True, stop=False)
                            mm(hv[:, r], wi_w[:, 0, r], lo[:, 2 * b:2 * b + 2], start=False, stop=False)
                            last = mm(hv[:, r], wi_w[:, 0, r], hi[:, 2 * b:2 * b + 2], start=False, stop=True)
                        last.then_inc(in_done, 1)
                output(0)
                if real(i - 2):
                    pe.wait_ge(wuse_ready, i - 1)
                    if since(i, 3):
                        pe.wait_ge(hF_ready, 2 * i - 4)
                    for b in range(2):
                        pe.wait_ge(h0_ready, 2 * i - 3 + b)
                        for g in range(2 * b, 2 * b + 2):
                            last = mm(E_H[second + b][:, (g % 2) * GC:(g % 2 + 1) * GC], wuse[:, 0, par * GROUPS + g, 0:HID],
                                      hid0[:, g * GC:(g + 1) * GC], start=True, stop=True)
                        last.then_inc(l1_done, 1)
                if par == 1 and real(i):
                    turn(i)
                output(1)
                if real(i - 2):
                    for b in range(2):
                        pe.wait_ge(h1_ready, 2 * i - 3 + b)
                        for g in range(2 * b, 2 * b + 2):
                            last = mm(E_H[first + b][:, (g % 2) * GC:(g % 2 + 1) * GC], wuse[:, 1, par * GROUPS + g, 0:HID],
                                      hid1[:, g * GC:(g + 1) * GC], start=True, stop=True)
                        last.then_inc(l2_done, 1)

            steps(pe, 4, 4, route_experts, 2 * FRONT)

        @block.scalar
        def _(act):
            f = nc.scalar.activation

            def tokenize(i, k):
                other = 1 - k
                if real(i - 2):
                    act.wait_ge(normed, i - 1)
                    f(cols(rows, i - 2), xh[:, k], ACT.Copy).then_inc(in_rows, 1)
                if real(i - 1):
                    act.wait_ge(centred, i)
                    if since(i, 2):
                        act.wait_ge(sq_summed, i - 1)
                    f(sq, cen[:, other], ACT.Square).then_inc(squared, 1)
                if real(i - 2):
                    act.wait_ge(back_turned, i - 1)
                    f(cols(x_hi, i - 2), P_X[:, :], ACT.Copy).then_inc(hi_stored, 1)
                if real(i - 1):
                    act.wait_ge(sq_summed, i)
                    f(stats[:, 2, other, 0:NJ], stats[:, 1, other, 0:NJ], ACT.Sqrt, bias=eps[:, 0:1], scale=1 / D
                      ).then_inc(rooted, 1)
                if real(i):
                    act.wait_ge(even_done, i + 1)
                    if since(i, 2):
                        act.wait_ge(added, i - 1)
                    f(odd_s[0:64, k], P_EVEN[0:64, :], ACT.Copy)
                    f(odd_s[64:128, k, 0:COLS - V], P_EVEN[64:128, V:], ACT.Copy).then_inc(odd_out, 1)

            act.wait_ge(zeroed, 1)
            tokenize(0, 0)
            act.wait_ge(setup_pe, 1)
            act.wait_ge(setup_pool, 1)
            for h in range(2):
                part = slice(64 * h, 64 * h + 64)
                last = f(z_w[part, 0, :, 64 * h:64 * h + 64], by(P_W[part, 0:128], 64), ACT.Copy)
            last.then_inc(setup_act, 1)
            steps(act, 1, 2, tokenize, done=1)

            def learn(i, k):
                other = 1 - k
                if real(i):
                    act.wait_ge(z0_done, i + 1)
                    if since(i, 2):
                        act.wait_ge(s0t_done, i - 1)
                        act.wait_ge(z1_done, i - 1)
                        act.wait_ge(c0_done, i - 1)
                        act.wait_ge(dz0_done, i - 1)
                        act.wait_ge(ss_done, i - 1)
                    f(s0[:, k], A_Z0[:, :], ACT.Silu, bias=w["b0_dd"]).then_inc(s0_done, 1)
                    f(c0[:, k], A_Z0[:, :], ACT.Tanh, bias=half_b[:, 0:1], scale=0.5).then_inc(t0_done, 1)
                if real(i - 1):
                    act.wait_ge(s0t_done, i)
                    if since(i, 3):
                        act.wait_ge(gw_done, i - 2)
                    f(factors[:, other, :, D:2 * D], by(A_S0T[:, :], D), ACT.Copy).then_inc(s0t_out, 1)
                if real(i):
                    act.wait_ge(z1_done, i + 1)
                    if since(i, 2):
                        act.wait_ge(c1_done, i - 1)
                        act.wait_ge(dz1t_done, i - 1)
                    f(s1[:, k], A_Z1[:, :], ACT.Silu, bias=w["b1_dd"]).then_inc(s1_done, 1)
                    f(c1[:, k], A_Z1[:, :], ACT.Tanh, bias=half_b[:, 1:2], scale=0.5).then_inc(t1_done, 1)
                if real(i - 1):
                    f(factors[:, other, :, 0:D], by(cols(rows, i - 1), D), ACT.Copy).then_inc(x_out, 1)

            learn(0, 0)
            tokenize(B + 1, 1)
            act.wait_ge(ones_set, 1)
            act.wait_ge(in_rows, B)
            learn(1, 1)
            act.wait_ge(logit_done, B)
            f(alr[:, :, 0], logit[:, :], ACT.Tanh, bias=half_b[:, 2:3], scale=0.5).then_inc(alr_t, 1)
            steps(act, 1, 2, learn, done=2)

            def retrieve(i, k):
                other = 1 - k
                if real(i):
                    act.wait_ge(rz0_done, i + 1)
                    if since(i, 2):
                        act.wait_ge(y1_done, i - 1)
                    f(p0[:, k], R_Z0[k][:, :], ACT.Silu, bias=params[:, 128:129]).then_inc(p0_done, 1)
                if real(i - 1):
                    act.wait_ge(rz1_done, i)
                    if since(i, 3):
                        act.wait_ge(hs_done, i - 2)
                    f(p1[:, other], R_Z1[:, :], ACT.Silu, bias=params[:, 129:130]).then_inc(p1_done, 1)
                if k == 0 and since(i, 4):
                    for q in range(2):
                        act.wait_ge(h2t_done, i - 3 + q)
                        f(cols(resid, i - 4 + q), R_T[q][:, :], ACT.Copy).then_inc(h2t_out, 1)

            steps(act, 0, 2, retrieve)

            act.wait_ge(centred2, 1)
            f(sq2, cen2, ACT.Square).then_inc(squared2, 1)
            retrieve(B, 0)
            act.wait_ge(sq_summed2, 1)
            f(stats[:, 2, 0], stats[:, 1, 0], ACT.Sqrt, bias=eps[:, 0:1], scale=1 / D).then_inc(rooted2, 1)
            retrieve(B + 2, 0)
            act.wait_ge(h2t_done, B)

            def route_experts(i, k):
                par = k % 2
                first, second = 2 * par, 2 * (1 - par)
                if real(i - 2):
                    if since(i, 3):
                        act.wait_ge(l1_done, 2 * i - 4)
                    for b in range(2):
                        act.wait_ge(in_done, 2 * i - 3 + b)
                        f(hid0[:, b * COLS:(b + 1) * COLS], E_H[first + b][:, :], ACT.Relu, bias=w["bi"]
                          ).then_inc(h0_ready, 1)
                    if since(i, 3):
                        act.wait_ge(l2_done, 2 * i - 4)
                    for b in range(2):
                        act.wait_ge(l1_done, 2 * i - 3 + b)
                        for g in range(2 * b, 2 * b + 2):
                            last = f(hid1[:, g * GC:(g + 1) * GC], E_H[second + b][:, (g % 2) * GC:(g % 2 + 1) * GC],
                                     ACT.Relu, bias=wuse[:, 0, par * GROUPS + g, HID:WE])
                        last.then_inc(h1_ready, 1)
                if par == 0 and real(i) and since(i, 2):
                    act.wait_ge(centred2, i // 2 + 1)
                    act.wait_ge(sq_summed2, i // 2)
                    f(sq2, cen2, ACT.Square).then_inc(squared2, 1)
                if par == 1 and real(i):
                    for q in range(2):
                        act.wait_ge(turned2, i + q)
                        if since(i, 5):
                            act.wait_ge(in_done, 2 * i - 6)
                        f(half_of(x2_hi, k, q), E_X[q][:, :], ACT.Copy).then_inc(x2_hi_done, 1)
                if real(i - 2):
                    if since(i, 6):
                        act.wait_ge(wo_done, i - 4 - par)
                    for b in range(2):
                        act.wait_ge(l2_done, 2 * i - 3 + b)
                        for g in range(2 * b, 2 * b + 2):
                            src = E_H[first + b][:, (g % 2) * GC:(g % 2 + 1) * GC]
                            dst = hidF[:, ((k + 2) % 4) // 2].rearrange("p (j r) (b g v) -> p b g r j v", r=2, b=2, g=GROUPS)
                            last = f(dst[:, par, g], src.rearrange("p (r j v) -> p r j v", r=2, v=GV), ACT.Relu,
                                     bias=wuse[:, 1, par * GROUPS + g, HID:WE])
                        last.then_inc(hF_ready, 1)
                if par == 0 and real(i) and since(i, 2):
                    act.wait_ge(sq_summed2, i // 2 + 1)
                    f(stats[:, 2, 0], stats[:, 1, 0], ACT.Sqrt, bias=eps[:, 0:1], scale=1 / D).then_inc(rooted2, 1)

            steps(act, 2, 4, route_experts, 2 * FRONT)

        @block.vector
        def _(dve):
            tt, stt, ts = nc.vector.tensor_tensor, nc.vector.scalar_tensor_tensor, nc.vector.tensor_scalar
            reduce = nc.vector.tensor_reduce

            def each(a):
                return a.rearrange("p (n o) -> p n o", o=1).to_broadcast([128, a.shape[1], D])

            dve.wait_ge(fold_pe, 1)
            copy = nc.vector.tensor_copy
            for q, folds in enumerate((3, 3, FOLDS - 6)):
                at_q = slice(3 * q * FOLD_OUT, (3 * q + folds) * FOLD_OUT)
                made = F_W[q][:, 0:folds * FOLD_W].rearrange("p (g k o) -> p g k o", g=folds, o=FOLD_OUT)
                for h in range(2):
                    part = slice(64 * h, 64 * h + 64)
                    for half in range(2):
                        k = half * STRIDE + h * HALF
                        last = copy(patch_w[part, :, half, at_q].rearrange("p t (g o) -> p g t o", o=FOLD_OUT),
                                    made[part, :, k:k + HALF])
                copy(patch_end[64:128, D:][:, at_q].rearrange("p (g o) -> p g o", o=FOLD_OUT),
                     made[64:128, :, 2 * STRIDE])
            last.then_inc(folded, 1)
            dve.wait_ge(folded, 1)
            copy(patch_end[:, 0:D], patch_w[:, HALF - 1, 0])
            copy(patch_end[0:64, D:], patch_w[0:64, HALF - 1, 1]).then_inc(folded, 1)
            copy(patch_w[:, :, 2], patch_w[:, :, 0]).then_inc(folded, 1)
            dve.wait_ge(zeroed, 1)

            def tokenize(i, k):
                other = 1 - k
                if real(i - 1):
                    total, sq_total, root, rate = (stats[:, n, other, 0:NJ] for n in range(4))
                    tokens = by(P_H[:, :], D)
                    dve.wait_ge(turned, i)
                    if since(i, 3):
                        dve.wait_ge(centred, i - 2)
                    reduce(total, tokens, AX.X, ALU.add).then_inc(summed, 1)
                    dve.wait_ge(summed, i)
                    if since(i, 3):
                        dve.wait_ge(squared, i - 2)
                        dve.wait_ge(normed, i - 2)
                    stt(by(cen[:, other], D), each(total), -1 / D, tokens, ALU.mult, ALU.add).then_inc(centred, 1)
                    dve.wait_ge(squared, i)
                    if since(i, 3):
                        dve.wait_ge(rooted, i - 2)
                    reduce(sq_total, by(sq, D), AX.X, ALU.add).then_inc(sq_summed, 1)
                    dve.wait_ge(rooted, i)
                    if since(i, 3):
                        dve.wait_ge(normed, i - 2)
                    nc.vector.reciprocal(rate, root).then_inc(rate_done, 1)
                    dve.wait_ge(rate_done, i)
                    dve.wait_ge(centred, i)
                    if since(i, 3):
                        dve.wait_ge(back_turned, i - 2)
                        dve.wait_ge(in_rows, i - 2)
                        dve.wait_ge(xlr_done, i - 2)
                    tt(by(xh[:, other], D), by(cen[:, other], D), each(rate), ALU.mult).then_inc(normed, 1)
                if real(i - 2):
                    dve.wait_ge(xlr_done, i - 1)
                    reduce(cols(logit, i - 2, 2 * TILES), by(xlr, D), AX.X, ALU.add).then_inc(logit_done, 1)
                    dve.wait_ge(hi_stored, i - 1)
                    tt(cols(x_lo, i - 2), P_X[:, :], cols(x_hi, i - 2), ALU.subtract).then_inc(stored, 1)
                if real(i):
                    dve.wait_ge(odd_done, i + 1)
                    dve.wait_ge(odd_out, i + 1)
                    if since(i, 2):
                        dve.wait_ge(turned, i - 1)
                        dve.wait_ge(kept, i - 1)
                    tt(h_new[:, k], P_ODD[k][:, :], odd_s[:, k], ALU.add).then_inc(added, 1)

            tokenize(0, 0)
            dve.wait_ge(route_in, 16)
            nc.vector.tensor_copy(route_f[:, 0], route_sb[:]).then_inc(route_step, 1)
            dve.wait_ge(route_step, 1)
            ts(route_f[:, 1], route_f[:, 0], 0.0, None, ALU.is_ge).then_inc(route_step, 1)
            ts(route_f[:, 2], route_f[:, 0], float(EXPERTS), -1.0, ALU.subtract, ALU.mult).then_inc(route_step, 1)
            dve.wait_ge(route_step, 3)
            stt(route_f[:, 3], route_f[:, 0], float(EXPERTS), route_f[:, 1], ALU.is_lt, ALU.mult).then_inc(route_step, 1)
            dve.wait_ge(route_step, 4)
            tt(route_f[:, 1], route_f[:, 2], route_f[:, 3], ALU.mult).then_inc(route_step, 1)
            dve.wait_ge(route_step, 5)
            ts(route_ix[:], route_f[:, 1], -1.0, float(EXPERTS), ALU.mult, ALU.add).then_inc(route_step, 1)

            dve.wait_ge(setup_act, 1)
            for h in range(2):
                part, at_h = slice(64 * h, 64 * h + 64), slice(64 * h, 64 * h + 64)
                last = tt(z_w[part, 1, :, at_h], by(P_W[part, 0:128], 64), z_w[part, 0, :, at_h], ALU.subtract)
            last.then_inc(split_done, 1)
            steps(dve, 1, 2, tokenize, done=1)

            def learn(i, k):
                other = 1 - k

                def turned_out_of(src, c, half):
                    return tt(dzt[:, half[0], :, half[1] * D:(half[1] + 1) * D], by(src[:, :], D),
                              alr[:, bass.ds(c * 2 * TILES, 2 * TILES), :].to_broadcast([128, 2 * TILES, D]), ALU.mult)

                def twice_derivative(s, c, made, done):
                    stt(c[:, k], s[:, k], 1.0, c[:, k], ALU.subtract, ALU.mult).then_inc(made, 1)
                    dve.wait_ge(made, i + 1)
                    return stt(c[:, k], s[:, k], 1.0, c[:, k], ALU.add, ALU.subtract).then_inc(done, 1)

                if real(i - 2):
                    dve.wait_ge(dz0t_done, i - 1)
                    if since(i, 4):
                        dve.wait_ge(gw_done, i - 3)
                    turned_out_of(A_DZ0T, i - 2, (k, 0)).then_inc(dz0t_out, 1)
                if real(i):
                    dve.wait_ge(t0_done, i + 1)
                    twice_derivative(s0, c0, m0_done, c0_done)
                    dve.wait_ge(t1_done, i + 1)
                    twice_derivative(s1, c1, m1_done, c1_done)
                if real(i - 1):
                    dve.wait_ge(back_done, i)
                    dve.wait_ge(dz1_done, i)
                    stt(dd[:, other], A_BACK[:, :], 0.5, dd[:, other], ALU.mult, ALU.add).then_inc(dy_done, 1)
                if real(i):
                    dve.wait_ge(d_done, i + 1)
                    dve.wait_ge(ss_done, i + 1)
                    tt(dd[:, k], A_D[:, :], dd[:, k], ALU.add).then_inc(dd_done, 1)
                    dve.wait_ge(dd_done, i + 1)
                    dve.wait_ge(c1_done, i + 1)
                    tt(c1[:, k], dd[:, k], c1[:, k], ALU.mult).then_inc(dz1_done, 1)
                if isinstance(i, int) and i == 1:
                    dve.wait_ge(alr_t, 1)
                    ts(alr[:, :, 0], alr[:, :, 0], MAX_ALR / D / 2, MAX_ALR / D / 2, ALU.mult, ALU.add).then_inc(alr_done, 1)
                    dve.wait_ge(alr_done, 1)
                if real(i - 1):
                    dve.wait_ge(dz1t_done, i)
                    if since(i, 3):
                        dve.wait_ge(gw_done, i - 2)
                    turned_out_of(A_DZ1T, i - 1, (other, 1)).then_inc(dz1t_out, 1)

            learn(0, 0)
            tokenize(B + 1, 1)
            steps(dve, 2, 2, learn, done=1)

            old = W[:, AT["w0_dd"][0]:AT["b1_dd"][1]]
            dve.wait_ge(gw_done, B)
            nc.vector.tensor_copy(grad_s[:, :], A_G[:, 0:XW]).then_inc(learn_dve, 1)
            dve.wait_ge(learn_pe, 1)
            nc.vector.tensor_copy(gradt_s[:, :], A_Z0[:, 0:128]).then_inc(learn_dve, 1)
            dve.wait_ge(learn_pe, 2)
            g = A_Z1[:, 0:130]
            nc.vector.tensor_copy(adam[:, 0], g).then_inc(learn_dve, 1)
            dve.wait_ge(learn_dve, 3)
            stt(adam[:, 1], adam[:, 0], -1.0, adam[:, 0], ALU.mult, ALU.max).then_inc(learn_dve, 1)
            dve.wait_ge(learn_dve, 4)
            ts(adam[:, 1], adam[:, 1], ADAM_EPS, None, ALU.add).then_inc(learn_dve, 1)
            dve.wait_ge(learn_dve, 5)
            nc.vector.reciprocal(adam[:, 2], adam[:, 1]).then_inc(learn_dve, 1)
            dve.wait_ge(learn_dve, 6)
            stt(adam[:, 0], adam[:, 0], -LR, adam[:, 2], ALU.mult, ALU.mult).then_inc(learn_dve, 1)
            dve.wait_ge(learn_dve, 7)
            stt(params[:, :], old, 1.0 - LR * WD, adam[:, 0], ALU.mult, ALU.add).then_inc(learn_dve, 1)
            blocks = [(slice(64 * h, 64 * h + 64), slice(64 * h, 64 * h + 64)) for h in range(2)]
            dve.wait_ge(learn_pe, 3)
            for part, at_h in blocks:
                nc.vector.tensor_copy(r_w[part, 0, at_h], A_S0T[part, 0:D]).then_inc(learn_dve, 1)
            dve.wait_ge(learn_dve, 10)
            for part, at_h in blocks:
                tt(r_w[part, 1, at_h], A_S0T[part, 0:D], r_w[part, 0, at_h], ALU.subtract).then_inc(learn_dve, 1)
            for part, at_h in blocks:
                nc.vector.tensor_copy(n1_bd[part, at_h], params[part, 64:128]).then_inc(learn_dve, 1)

            def retrieve(i, k):
                par = k % 2
                if real(i):
                    dve.wait_ge(rq_done, i + 1)
                    dve.wait_ge(p0_done, i + 1)
                    if since(i, 2):
                        dve.wait_ge(rz1_done, i - 1)
                        dve.wait_ge(h2_done, i - 1)
                    tt(y1[:, par], R_Q[par][:, :], p0[:, par], ALU.add).then_inc(y1_done, 1)
                if real(i - 1):
                    dve.wait_ge(hs_done, i)
                    dve.wait_ge(y1_done, i)
                    if since(i, 5):
                        dve.wait_ge(h2t_done, i - 4 + par)
                    tt(h2_of((k - 1) % 4), by(hs[:, 1 - par], V), by(y1[:, 1 - par], V), ALU.add).then_inc(h2_done, 1)

            def tokens_of(i):
                return cols(resid, i // 2, NP * D).rearrange("p (n d) -> p n d", d=D)

            def sum_pair(i):
                if since(i, 2):
                    dve.wait_ge(centred2, i // 2)
                reduce(stats[:, 0, 0], tokens_of(i), AX.X, ALU.add).then_inc(summed2, 1)

            def centre_pair(i):
                dve.wait_ge(summed2, i // 2 + 1)
                if since(i, 2):
                    dve.wait_ge(normed2, i // 2)
                stt(cen2, each(stats[:, 0, 0]), -1 / D, tokens_of(i), ALU.mult, ALU.add).then_inc(centred2, 1)

            def sum_squares(i):
                dve.wait_ge(squared2, i // 2 + 1)
                reduce(stats[:, 1, 0], sq2, AX.X, ALU.add).then_inc(sq_summed2, 1)

            def scale_pair(i):
                dve.wait_ge(rooted2, i // 2 + 1)
                nc.vector.reciprocal(stats[:, 3, 0], stats[:, 2, 0]).then_inc(rate2_done, 1)
                dve.wait_ge(rate2_done, i // 2 + 1)
                dve.wait_ge(centred2, i // 2 + 1)
                if since(i, 2):
                    dve.wait_ge(turned2, i)
                tt(xh2, cen2, each(stats[:, 3, 0]), ALU.mult).then_inc(normed2, 1)

            steps(dve, -4, 4, retrieve, 2 * FRONT, end=B - 4)
            dve.wait_ge(h2t_out, 2)
            dve.wait_ge(normed, B)
            sum_pair(0)
            retrieve(B - 4, 0)
            centre_pair(0)
            for i in range(B - 3, B):
                retrieve(i, i % 4)
            sum_squares(0)
            retrieve(B, 0)
            scale_pair(0)
            dve.wait_ge(h2t_out, B)

            def route_experts(i, k):
                par = k % 2
                if par == 0 and real(i) and since(i, 2):
                    sum_pair(i)
                    centre_pair(i)
                if par == 1 and real(i):
                    for q in range(2):
                        dve.wait_ge(x2_hi_done, i + q)
                        tt(half_of(x2_lo, k, q), E_X[q][:, :], half_of(x2_hi, k, q), ALU.subtract).then_inc(x2_done, 1)
                if since(i, 4):
                    s = (k - par) // 2
                    if par == 0 and since(i, 8):
                        dve.wait_ge(out_dma[s], 8 * i - 32 - 16 * s)
                    dve.wait_ge(wo_done, i - 3)
                    if par == 0:
                        dve.wait_ge(biased, (i - 2) // 2)
                    tt(outs[:, s, par * COLS:(par + 1) * COLS], E_O[par][:, :], cols(resid, i - 4), ALU.add
                       ).then_inc(out_added, 1)
                if par == 0 and real(i) and since(i, 2):
                    sum_squares(i)
                    scale_pair(i)

            steps(dve, 4, 4, route_experts, 2 * FRONT)

        @block.gpsimd
        def _(pool):
            tt, ts = nc.gpsimd.tensor_tensor, nc.gpsimd.tensor_scalar

            def across(row, n):
                return row.rearrange("p (a d) -> p a d", a=1).to_broadcast([128, n, D])

            nc.gpsimd.memset(odd_s[:, :, COLS - V:], 0.0)
            nc.gpsimd.memset(eps[:], LN_EPS)
            for buffer in (z_w[:].bitcast(F32), r_w[:].bitcast(F32), n1_bd[:]):
                last = nc.gpsimd.memset(buffer, 0.0)
            last.then_inc(zeroed, 1)
            pool.wait_ge(w_in, 16)
            ts(half_b[:, 0:2], W[:, AT["b0_dd"][0]:AT["b1_dd"][1]], 0.5, 0.0, ALU.mult, ALU.add)
            ts(half_b[:, 2:3], w["blr"], 0.5, 0.0, ALU.mult, ALU.add)
            tt(key_value, w["wk_bd"], w["wv_bd"], ALU.subtract).then_inc(pool_split, 1)
            nc.gpsimd.tensor_copy(q_w[:, 0], w["wq_bd"]).then_inc(pool_split, 1)
            pool.wait_ge(pool_split, 1)
            nc.gpsimd.tensor_copy(d_w[:, 0], key_value).then_inc(pool_split, 1)
            pool.wait_ge(pool_split, 3)
            tt(q_w[:, 1], w["wq_bd"], q_w[:, 0], ALU.subtract)
            tt(d_w[:, 1], key_value, d_w[:, 0], ALU.subtract)
            wi = W[:, AT["wi0"][0]:AT["wi1"][1]]
            nc.gpsimd.tensor_copy(wi_w[:, 0].rearrange("p r n -> p (r n)"), wi).then_inc(pool_split, 1)
            pool.wait_ge(pool_split, 4)
            tt(wi_w[:, 1].rearrange("p r n -> p (r n)"), wi, wi_w[:, 0].rearrange("p r n -> p (r n)"), ALU.subtract)
            for name in ("ws0", "ws1"):
                last = tt(w[name][:, 0:HID], w[name][:, 0:HID], w["ident"], ALU.add)
            last.then_inc(setup_pool, 1)

            def tokenize(i, k):
                other = 1 - k
                if real(i):
                    pool.wait_ge(added, i + 1)
                    nc.gpsimd.tensor_copy(cols(hT, i), h_new[:, k]).then_inc(kept, 1)
                if real(i - 1):
                    pool.wait_ge(normed, i)
                    if since(i, 2):
                        pool.wait_ge(logit_done, i - 1)
                    tt(by(xlr, D), by(xh[:, other], D), across(w["wlr_row"], NJ), ALU.mult).then_inc(xlr_done, 1)

            steps(pool, 1, 2, tokenize)

            pool.wait_ge(normed, B)
            nc.gpsimd.memset(factors[:, :, :, 2 * D:], 1.0).then_inc(ones_set, 1)

            def learn(i, k):
                other = 1 - k
                if real(i):
                    pool.wait_ge(s1_done, i + 1)
                    if since(i, 2):
                        pool.wait_ge(dz0_done, i - 1)
                    tt(dd[:, k], s0[:, k], s1[:, k], ALU.add).then_inc(ss_done, 1)
                if real(i - 1):
                    pool.wait_ge(dy_done, i)
                    pool.wait_ge(c0_done, i)
                    if since(i, 3):
                        pool.wait_ge(dz0t_done, i - 2)
                    tt(dz0[:, other], dd[:, other], c0[:, other], ALU.mult).then_inc(dz0_done, 1)

            steps(pool, 1, 2, learn)

            def retrieve(i, k):
                par = k % 2
                if real(i - 1):
                    pool.wait_ge(p1_done, i)
                    if since(i, 3):
                        pool.wait_ge(h2_done, i - 2)
                    tt(hs[:, 1 - par], cols(hT, i - 1), p1[:, 1 - par], ALU.add).then_inc(hs_done, 1)

            steps(pool, 1, 2, retrieve)

            pool.wait_ge(wr_in, 16)
            pool.wait_ge(hs_done, B)
            pool.wait_ge(route_step, 6)

            def route_experts(i, k):
                if real(i):
                    if since(i, 2):
                        pool.wait_ge(l2_done, 2 * i - 2)
                        pool.wait_ge(hF_ready, 2 * i - 2)
                    for g in range(GROUPS):
                        e = pool.value_load(route_ix[0:1, bass.ds(i * GROUPS + g, 1)], min_val=0, max_val=EXPERTS)
                        for l, name in enumerate(("ws0", "ws1")):
                            last = tt(wuse[:, l, k * GROUPS + g], wr[:, l, bass.ds(e, 1)].rearrange("p o n -> p (o n)"),
                                      w[name], ALU.add)
                    last.then_inc(wuse_ready, 1)

                if k % 2 == 1:
                    pool.wait_ge(centred2, (i + 1) // 2)
                    pair = cols(resid, (i - 1) // 2, NP * D).rearrange("p (n d) -> p n d", d=D)
                    tt(pair, pair, across(w["bo"], NP), ALU.add).then_inc(biased, 1)

            steps(pool, 0, 2, route_experts)


def packed(inputs):
    def f(name):
        return np.asarray(inputs[name])

    eye, zero = np.eye(64, dtype=np.float32), np.zeros((64, 64), np.float32)

    def bd(a):
        return np.block([[a, zero], [zero, a]])

    def down(a):
        return np.concatenate([a, a], 0)

    wk, wq, wv, w1 = f("L0_attn_Wk"), f("L0_attn_Wq"), f("L0_attn_Wv"), f("L0_attn_Ws")[1]
    wlr = f("L0_attn_Wlr")
    ws, bs = f("L0_ffn_Ws"), f("L0_ffn_bs")
    wi, none = f("L0_ffn_Wi"), np.zeros((D, HID), np.float32)
    parts = {
        "wk_bd": bd(wk), "wv_bd": bd(wv), "wq_bd": bd(wq), "w1_bd": bd(w1), "w1t_bd": bd(w1.T),
        "wkt_dd": np.block([[wk.T, wk.T], [zero, zero]]), "wqt_dd": np.block([[wq.T, wq.T], [zero, zero]]),
        "grad0": np.block([[wk, wk], [zero, zero]]), "grad1": np.block([[wk, wk], [eye, eye]]),
        "w0_dd": down(f("L0_attn_Ws")[0]), "w1_dd": down(w1),
        "b0_dd": down(f("L0_attn_bs")[0][:, None]), "b1_dd": down(f("L0_attn_bs")[1][:, None]),
        "wlr_row": np.tile(wlr.T, (128, 1)),
        "blr": np.tile(f("L0_attn_blr")[None, :], (128, 1)),
        "wi0": np.concatenate([wi.T, none], 0), "wi1": np.concatenate([none, wi.T], 0),
        "bi": f("L0_ffn_bi")[:, None],
        "ws0": np.concatenate([ws[0, 0].T, bs[0, 0][:, None]], 1),
        "ws1": np.concatenate([ws[1, 0].T, bs[1, 0][:, None]], 1),
        "wot": f("L0_ffn_Wo").T, "bo": np.tile(f("L0_ffn_bo")[None, :], (128, 1)),
        "ident": np.eye(128, dtype=np.float32),
        "spread0": np.block([[eye, eye], [zero, zero]]), "spread1": np.block([[zero, zero], [eye, eye]]),
    }
    return np.ascontiguousarray(np.concatenate([parts[n] for n, _ in PACK], 1))


def kernel(**inputs):
    import concourse.bacc as bacc
    from concourse.bass_utils import run_bass_kernel_spmd

    tokw = np.asarray(inputs["L0_tok_W"]).reshape(D, 2, PATCH // 2 + 1, C)
    tokw = np.stack([tokw[:, part, f] for part, f in COEFS], 1).reshape(FOLDS, FOLD_OUT, len(COEFS), C)
    tokw = tokw.transpose(2, 1, 0, 3)
    tokw = np.concatenate([tokw, tokw], 3).reshape(128, -1)
    wr, br = np.asarray(inputs["L0_ffn_Wr"]), np.asarray(inputs["L0_ffn_br"])
    experts = np.zeros((HID, LAYERS, EXPERTS + 1, WE), wr.dtype)
    experts[:, :, :EXPERTS, :HID] = wr.transpose(3, 0, 1, 2)
    experts[:, :, :EXPERTS, HID] = br.transpose(2, 0, 1)
    arrays = {
        "x": np.ascontiguousarray(inputs["x"]),
        "tokw": np.concatenate([tokw, fold_table()], 1),
        "pack": packed(inputs),
        "experts": experts.reshape(HID, -1),
        "route": np.ascontiguousarray(inputs["L0_ffn_route_id"]).reshape(1, -1),
    }
    nc = bacc.Bacc("TRN2", target_bir_lowering=False, num_devices=1)
    args = [nc.dram_tensor(n, a.shape, mybir.dt.from_np(a.dtype), kind="ExternalInput").ap()
            for n, a in arrays.items()]
    out = nc.dram_tensor("out", (B, V * NP, D), F32, kind="ExternalOutput").ap()
    tower(nc, *args, out)
    r = run_bass_kernel_spmd(nc, [arrays], core_ids=[0])
    return r.results[0]["out"]
```
